# Optimizing a Trainium2 kernel written in Bass

```python
import numpy as np
import jax
import jax.numpy as jnp

def _softmax(x, axis=-1):
    return jax.nn.softmax(x, axis=axis)

def _gelu(x):
    return jax.nn.gelu(x, approximate=True)

def _silu(x):
    return jax.nn.silu(x)

def _sigmoid(x):
    return jax.nn.sigmoid(x)

def _layernorm(x, axis=-1, eps=1e-05):
    m = jnp.mean(x, axis=axis, keepdims=True)
    v = jnp.var(x, axis=axis, keepdims=True)
    return (x - m) / jnp.sqrt(v + eps)

def _scatter_add(tgt, idx, src, axis=0):
    return tgt.at[idx].add(src)

def _segment_sum(src, seg, n):
    return jax.ops.segment_sum(src, seg, n)
kernel_name = 'mk_gnn_resnorm_d2_gnn_r32_48600b'

def setup_inputs(seed: int=0):
    np.random.seed(seed)
    _w = jnp.asarray

    def _rec_inputs():
        import jax
        import jax.numpy as jnp
        _gk = jax.random.key(seed)
        x = -0.000202 + 1 * jax.random.normal(jax.random.fold_in(_gk, 1), (50000, 128), jnp.float32)
        src = jax.random.randint(jax.random.fold_in(_gk, 2), (50000,), 0, 50000, jnp.int32)
        dst = jax.random.randint(jax.random.fold_in(_gk, 3), (50000,), 0, 50000, jnp.int32)
        _o = jnp.argsort(dst, stable=True)
        src = src[_o]
        dst = dst[_o]
        edge_type_32 = jax.random.randint(jax.random.fold_in(_gk, 14), (50000,), 0, 32, jnp.int32)
        return (x, src, dst, edge_type_32)
    x, src, dst, edge_type_32 = _rec_inputs()

    def _L0_gnn_setup():
        import jax, jax.numpy as jnp
        import numpy as np
        N = 50000
        E = 25000
        IN = 128
        OUT = 128
        H = 4
        C = OUT // H
        G = 64
        NEG_SLOPE = 0.2
        GN_EPS = 1e-05
        key = jax.random.key(seed)
        ks = jax.random.split(key, 6)
        x = jax.random.normal(ks[0], (N, IN), dtype=jnp.float32)
        edge_index = jax.random.randint(ks[1], (2, E), 0, N, dtype=jnp.int32)
        batch = jnp.sort(jax.random.randint(ks[2], (N,), 0, G, dtype=jnp.int32))
        s = float(np.sqrt(6.0 / (IN + H * C)))
        Wl = jax.random.uniform(ks[3], (IN, H * C), jnp.float32, -s, s)
        Wr = jax.random.uniform(ks[4], (IN, H * C), jnp.float32, -s, s)
        sa = float(np.sqrt(6.0 / (C + 1)))
        att = jax.random.uniform(ks[5], (H, C), jnp.float32, -sa, sa)
        bias_conv = jnp.zeros((H * C,), jnp.float32)
        gn_weight = jnp.ones((OUT,), jnp.float32)
        gn_bias = jnp.zeros((OUT,), jnp.float32)
        gn_mean_scale = jnp.ones((OUT,), jnp.float32)
        return {'x': x, 'edge_index': edge_index, 'batch': batch, 'Wl': Wl, 'Wr': Wr, 'att': att, 'bias_conv': bias_conv, 'gn_weight': gn_weight, 'gn_bias': gn_bias, 'gn_mean_scale': gn_mean_scale}
    _L0_gnn_all = _L0_gnn_setup()
    _L0_gnn_in = {k: v for k, v in _L0_gnn_all.items() if k in ('Wl', 'Wr', 'att', 'bias_conv', 'gn_weight', 'gn_bias', 'gn_mean_scale')}
    del _L0_gnn_all

    def _L1_gnn_setup():
        import jax, jax.numpy as jnp
        import numpy as np
        N_NODES = 3125
        N_EDGES = 50000
        D = 128
        N_RELS = 32
        N_BASES = 4
        N_LAYERS = 2
        key = jax.random.key(seed)
        ks = jax.random.split(key, 8)
        feat = jax.random.normal(ks[0], (N_NODES, D), dtype=jnp.float32)
        src = jax.random.randint(ks[1], (N_EDGES,), 0, N_NODES, dtype=jnp.int32)
        dst = jax.random.randint(ks[2], (N_EDGES,), 0, N_NODES, dtype=jnp.int32)
        etype = jax.random.randint(ks[3], (N_EDGES,), 0, N_RELS, dtype=jnp.int32)
        scale = 1.0 / np.sqrt(D)
        basis = jax.random.normal(ks[4], (N_LAYERS, N_BASES, D, D), dtype=jnp.float32) * scale
        comp = jax.random.normal(ks[5], (N_LAYERS, N_RELS, N_BASES), dtype=jnp.float32)
        loop_w = jax.random.normal(ks[6], (N_LAYERS, D, D), dtype=jnp.float32) * scale
        bias = jnp.zeros((N_LAYERS, D), dtype=jnp.float32)
        return {'feat': feat, 'src': src, 'dst': dst, 'etype': etype, 'basis': basis, 'comp': comp, 'loop_w': loop_w, 'bias': bias}
    _L1_gnn_all = _L1_gnn_setup()
    _L1_gnn_in = {k: v for k, v in _L1_gnn_all.items() if k in ('basis', 'comp', 'loop_w', 'bias')}
    del _L1_gnn_all
    return {'x': x, 'src': src, 'dst': dst, 'edge_type_32': edge_type_32, 'L0_gnn_Wl': _L0_gnn_in['Wl'], 'L0_gnn_Wr': _L0_gnn_in['Wr'], 'L0_gnn_att': _L0_gnn_in['att'], 'L0_gnn_bias_conv': _L0_gnn_in['bias_conv'], 'L0_gnn_gn_weight': _L0_gnn_in['gn_weight'], 'L0_gnn_gn_bias': _L0_gnn_in['gn_bias'], 'L0_gnn_gn_mean_scale': _L0_gnn_in['gn_mean_scale'], 'L1_gnn_basis': _L1_gnn_in['basis'], 'L1_gnn_comp': _L1_gnn_in['comp'], 'L1_gnn_loop_w': _L1_gnn_in['loop_w'], 'L1_gnn_bias': _L1_gnn_in['bias']}

def reference(x, src, dst, edge_type_32, L0_gnn_Wl, L0_gnn_Wr, L0_gnn_att, L0_gnn_bias_conv, L0_gnn_gn_weight, L0_gnn_gn_bias, L0_gnn_gn_mean_scale, L1_gnn_basis, L1_gnn_comp, L1_gnn_loop_w, L1_gnn_bias):
    import jax
    import jax.numpy as jnp

    def _L0_gnn_ref(x, edge_index, batch, Wl, Wr, att, bias_conv, gn_weight, gn_bias, gn_mean_scale):
        import jax, jax.numpy as jnp
        import numpy as np
        N = 50000
        E = 25000
        IN = 128
        OUT = 128
        H = 4
        C = OUT // H
        G = 64
        NEG_SLOPE = 0.2
        GN_EPS = 1e-05
        n = x.shape[0]
        loop = jnp.arange(n, dtype=edge_index.dtype)
        src = jnp.concatenate([edge_index[0], loop])
        dst = jnp.concatenate([edge_index[1], loop])
        xl = (x @ Wl).reshape(n, H, C)
        xr = (x @ Wr).reshape(n, H, C)
        m = xl[src] + xr[dst]
        e = jax.nn.leaky_relu(m, NEG_SLOPE)
        logits = jnp.einsum('ehc,hc->eh', e, att)
        amax = jax.ops.segment_max(logits, dst, num_segments=n)
        ex = jnp.exp(logits - amax[dst])
        denom = jax.ops.segment_sum(ex, dst, num_segments=n)
        alpha = ex / (denom[dst] + 1e-16)
        out = jax.ops.segment_sum(alpha[:, :, None] * xl[src], dst, num_segments=n)
        out = out.reshape(n, H * C) + bias_conv
        ones = jnp.ones((n, 1), out.dtype)
        cnt = jnp.maximum(jax.ops.segment_sum(ones, batch, num_segments=G), 1.0)
        mean = jax.ops.segment_sum(out, batch, num_segments=G) / cnt
        out_c = out - mean[batch] * gn_mean_scale
        var = jax.ops.segment_sum(out_c * out_c, batch, num_segments=G) / cnt
        y = out_c / jnp.sqrt(var[batch] + GN_EPS) * gn_weight + gn_bias
        return jax.nn.elu(y)

    def _L1_gnn_ref(feat, src, dst, etype, basis, comp, loop_w, bias):
        import jax, jax.numpy as jnp
        import numpy as np
        N_NODES = 3125
        N_EDGES = 50000
        D = 128
        N_RELS = 32
        N_BASES = 4
        N_LAYERS = 2
        n_nodes = feat.shape[0]
        n_layers, n_bases = (basis.shape[0], basis.shape[1])
        h = feat
        for l in range(n_layers):
            h_src = h[src]
            c = comp[l][etype]
            msg = c[:, 0:1] * (h_src @ basis[l, 0])
            for b in range(1, n_bases):
                msg = msg + c[:, b:b + 1] * (h_src @ basis[l, b])
            agg = jax.ops.segment_sum(msg, dst, num_segments=n_nodes)
            h = jnp.tanh(agg + h @ loop_w[l] + bias[l])
        return h
    edge_index = jnp.stack([src, dst])
    batch0 = jnp.zeros((50000,), jnp.int32)
    x = _layernorm(x + _L0_gnn_ref(x, edge_index, batch0, L0_gnn_Wl, L0_gnn_Wr, L0_gnn_att, L0_gnn_bias_conv, L0_gnn_gn_weight, L0_gnn_gn_bias, L0_gnn_gn_mean_scale), axis=-1)
    x = _layernorm(x + _L1_gnn_ref(x, src, dst, edge_type_32, L1_gnn_basis, L1_gnn_comp, L1_gnn_loop_w, L1_gnn_bias), axis=-1)
    return x

_drawn_inputs = setup_inputs


def setup_inputs(seed=0):
    import zlib

    import numpy as np

    out = dict(_drawn_inputs(seed))
    spreads = {'L0_gnn_bias_conv': (0.0, 0.51),
     'L0_gnn_gn_weight': (1.0, 0.2),
     'L0_gnn_gn_bias': (0.0, 0.1),
     'L0_gnn_gn_mean_scale': (1.0, 0.6),
     'L1_gnn_bias': (0.0, 0.1)}
    factors = {}
    for name, (base, spread) in spreads.items():
        noise = np.random.default_rng([zlib.crc32(name.encode()), seed]).standard_normal(out[name].shape)
        drawn = base * np.exp(spread * noise) if base else spread * noise
        out[name] = jnp.asarray(drawn.astype(out[name].dtype))
    for name, factor in factors.items():
        out[name] = (out[name] * factor).astype(out[name].dtype)
    return out
```

```python
from contextlib import ExitStack

import concourse.bass as bass
from concourse import mybir

F32 = mybir.dt.float32
I32 = mybir.dt.int32
ALU = mybir.AluOpType
ACT = mybir.ActivationFunctionType
AX = mybir.AxisListType

P = 128
D = 128
H = 4
C = D // H
BASES = 4
RELS = 32
LAYERS = 2
N = 50000
E = 50000

NT = 13
GROUP = NT * P
NG = N // GROUP
TAIL = N - NG * GROUP
LAST = NG // 2
NODE_TILES = NG * NT + 1

ET = 392
EG = 7
EGROUPS = ET // EG
EITER = EGROUPS // 2
FULL_E = (P - 1) * ET
REST_E = E - FULL_E

ROW = D + 2 * H
FAR = 65536
PAD_DST = 65535
LOW = 1e30
SLOPE = 0.2
EPS = 1e-5


def chunks(tiles):
    return [(c, t, min(4, tiles - t)) for c, t in enumerate(range(0, tiles, 4))]


def after(eng, sem, count):
    if not isinstance(count, int) or count > 0:
        eng.wait_ge(sem, count)


def wait_group(eng, bank_sems, i, s, tiles):
    eng.wait_ge(bank_sems[0], 4 * i + 2 * s + (2 if tiles > 8 else 1))
    if tiles > 4:
        eng.wait_ge(bank_sems[1], 4 * i + 2 * s + (2 if tiles > 12 else 1))


class Steps:

    def __init__(self, eng, sem):
        self.eng, self.sem, self.base, self.n, self.turns, self.per = eng, sem, 0, 0, None, 0

    def enter(self, turns, per):
        self.base, self.n, self.turns, self.per = self.base + self.n, 0, turns, per

    def leave(self, rounds):
        assert self.n == self.per, (self.n, self.per)
        self.base, self.n, self.turns = self.base + self.per * rounds, 0, None

    def did(self, ins):
        ins.then_inc(self.sem, 1)
        self.n += 1

    def wait(self):
        at = self.base + self.n
        self.eng.wait_ge(self.sem, at if self.turns is None else self.turns * self.per + at)


def in_pairs(eng, pair, rounds, steps=None):
    before = steps.n if steps else 0
    pair(0)
    per = steps.n - before if steps else 0
    with eng.Fori(1, rounds) as i:
        if steps:
            steps.enter(i - 1, per)
        pair(i)
    if steps:
        steps.leave(rounds - 1)


def node_groups(eng, body, steps=None):
    def pair(i):
        body(i, 0, P, NT)
        body(i, 1, P, NT)
    in_pairs(eng, pair, LAST, steps)
    body(LAST, 0, TAIL, 1)


def node_rows(dram, i, s, rows, tiles):
    if rows == P:
        part = dram[bass.ds((2 * i + s) * GROUP, GROUP), :]
    else:
        part = dram[NG * GROUP:N, :]
    return part.rearrange("(p t) d -> p (t d)", t=tiles)


def gnn_kernel(nc, x, src, dst, etype, Wl, Wr, att, bias_conv, gn_weight, gn_bias, gn_mean_scale,
               basis, comp, loop_w, bias, out):
    ctx = ExitStack()
    with ctx:
        def sb(name, shape, dt=F32):
            return ctx.enter_context(nc.sbuf_tensor(name, shape, dt))

        def sem(name):
            return ctx.enter_context(nc.semaphore(name))

        def sems(name):
            return [sem(f"{name}{k}") for k in range(2)]

        xl_d = nc.dram_tensor("xl_d", [N, D], F32).ap()
        xr_d = nc.dram_tensor("xr_d", [N, D], F32).ap()
        gat_d = nc.dram_tensor("gat_d", [N, ROW], F32).ap()
        conv_d = nc.dram_tensor("conv_d", [N, D], F32).ap()
        x1_d = nc.dram_tensor("x1_d", [N, D], F32).ap()
        agg_d = nc.dram_tensor("agg_d", [N, D], F32).ap()
        h1_d = nc.dram_tensor("h1_d", [N, D], F32).ap()

        src_i = sb("src_i", [P, ET], I32)
        dst_i = sb("dst_i", [P, ET], I32)
        next_i = sb("next_i", [P, ET], I32)
        etype_i = sb("etype_i", [P, ET], I32)
        xr_idx = sb("xr_idx", [P, ET], I32)
        out_idx = sb("out_idx", [P, ET], I32)
        cont = sb("cont", [P, ET])
        drop = sb("drop", [P, ET])
        coef = sb("coef", [P, LAYERS, ET, BASES])
        self_logit = sb("self_logit", [P, NODE_TILES, H])
        ident = sb("ident", [P, P])
        ones = sb("ones", [P, P])
        w_lr = sb("w_lr", [D, 2 * D])
        att_b = sb("att_b", [P, D])
        conv_b = sb("conv_b", [P, D])
        gnw_b = sb("gnw_b", [P, D])
        gnb_b = sb("gnb_b", [P, D])
        gms_b = sb("gms_b", [P, D])
        bias_b = sb("bias_b", [P, LAYERS, D])
        comp_b = sb("comp_b", [P, LAYERS, RELS, BASES])
        basis_s = sb("basis_s", [D, LAYERS, BASES, D])
        loop_s = sb("loop_s", [D, LAYERS, D])
        rel_id = sb("rel_id", [P, RELS])
        gn_scale = sb("gn_scale", [P, D])
        gn_shift = sb("gn_shift", [P, D])
        stat = sb("stat", [P, 6, D])
        next_last = sb("next_last", [P, 1], I32)
        after_next = sb("after_next", [P, 1], I32)
        last_f = sb("last_f", [P, 1])
        flag = sb("flag", [P, 4])
        fix_idx = sb("fix_idx", [P, 1], I32)
        edge_m = sb("edge_m", [P, 3, P])
        fix = sb("fix", [P, 2, ROW])
        fix_s = sb("fix_s", [P, 8, H])
        diag = sb("diag", [P, H, P])
        idx_st = sb("idx_st", [P, 2, 3, EG], I32)
        drop_st = sb("drop_st", [P, 2, EG])
        coef_st = sb("coef_st", [P, 2, EG, BASES + 1])
        logit = sb("logit", [P, EG, H])
        exp_in = sb("exp_in", [P, 2, EG, H])
        exp_out = sb("exp_out", [P, 2, EG, H])
        nexp_in = sb("nexp_in", [P, 2, NT, H])
        nexp_out = sb("nexp_out", [P, 2, NT, H])
        nsm = sb("nsm", [P, 3, NT, H])
        bn6 = sb("bn6", [P, NT, 6])
        bn2 = sb("bn2", [P, NT, 2])
        rstd = sb("rstd", [P, 2, NT])
        work = [sb(f"work{k}", [P, NT * ROW]) for k in range(14)]

        lr = sb("lr", [P, 2, NT, 2 * D])

        def tiles_of(k, tiles=NT, width=D):
            return work[k][:, 0:tiles * width].rearrange("p (t d) -> p t d", d=width)

        psum = [ctx.enter_context(nc.psum_tensor(f"bank{k}", [P, 512], F32)) for k in range(8)]

        cleared = sem("cleared")
        tables_in = sem("tables_in")
        weights_in = sem("weights_in")
        consts = sem("consts")
        tables_ok = sem("tables_ok")
        filled = sem("filled")
        fill_ready = sem("fill_ready")
        stage_done = sem("stage_done")
        passed = sem("passed")
        dve_steps = sem("dve_steps")
        pool_steps = sem("pool_steps")
        act_steps = sem("act_steps")

        x_in, x_used = sems("x_in"), sems("x_used")
        xt_ps, xt_cp = sems("xt_ps"), sems("xt_cp")
        lr_ps, l_cp, r_cp, l_read, lr_out = sems("lr_ps"), sems("l_cp"), sems("r_cp"), sems("l_read"), sems("lr_out")
        at_in, at_row, at_out = sems("at_in"), sems("at_row"), sems("at_out")
        at_arg, at_exp = sem("at_arg"), sem("at_exp")
        fix_rd, fix_mm, fix_act, fix_in, fix_out, fixed = (
            sem("fix_rd"), sem("fix_mm"), sem("fix_act"), sem("fix_in"), sem("fix_out"), sem("fixed"))
        ag_in, ag_used, cv_ok, cv_sq, cv_mm, cv_out = (
            sems("ag_in"), sems("ag_used"), sems("cv_ok"), sems("cv_sq"), sems("cv_mm"), sems("cv_out"))
        ag_arg, ag_exp = sem("ag_arg"), sem("ag_exp")
        zeroed, gn_var, gn_std, gn_ok = sem("zeroed"), sem("gn_var"), sem("gn_std"), sem("gn_ok")
        nx_in, nx_used, nx_ok, nx_out = sems("nx_in"), sems("nx_used"), sems("nx_ok"), sems("nx_out")
        nx_y, nx_e, nx_v, nx_r = sem("nx_y"), sem("nx_e"), sem("nx_v"), sem("nx_r")
        rel = []
        for l in range(LAYERS):
            rel.append({n: sems(f"r{l}_{n}") for n in (
                "h_in", "t_ps", "t_cp", "y_ps", "y_used", "row", "out",
                "n_in", "nt_ps", "nt_cp", "nm_ps", "nm_used", "s_ok", "h_ok", "z_ok", "nh_ok", "nh_out",
                )} | {n: sem(f"r{l}_{n}") for n in ("fix_in", "fix_out", "fix_mm", "fix_row", "v_ok", "r_ok")})

        def alone(eng):
            eng.sem_inc(passed, 1)

        def end_stage(eng, k):
            eng.drain().then_inc(stage_done, 1)
            eng.wait_ge(stage_done, 5 * k)

        block = ctx.enter_context(nc.Block())

        edge_rows = lambda a, o=0: a[o:o + FULL_E].rearrange("(p t) -> p t", t=ET)

        @block.sync
        def _(sp):
            sp.dma_start(w_lr[:, 0:D], Wl).then_inc(weights_in, 16)
            sp.dma_start(w_lr[:, D:2 * D], Wr).then_inc(weights_in, 16)
            for tile, row in ((att_b[:, :], att.rearrange("h c -> (h c)")), (conv_b[:, :], bias_conv),
                              (gnw_b[:, :], gn_weight), (gnb_b[:, :], gn_bias), (gms_b[:, :], gn_mean_scale),
                              (bias_b[:, :, :].rearrange("p l d -> p (l d)"), bias.rearrange("l d -> (l d)")),
                              (comp_b[:, :, :, :].rearrange("p l r b -> p (l r b)"),
                               comp.rearrange("l r b -> (l r b)"))):
                sp.dma_start(tile, row.partition_broadcast(P)).then_inc(weights_in, 16)
            sp.dma_start(basis_s[:, :, :, :], basis.rearrange("l b k n -> k l b n")).then_inc(weights_in, 16)
            sp.dma_start(loop_s[:, :, :], loop_w.rearrange("l k n -> k l n")).then_inc(weights_in, 16)
            sp.wait_ge(cleared, 6)
            for tile, a, o in ((src_i, src, 0), (dst_i, dst, 0), (etype_i, etype, 0), (next_i, dst, 1)):
                sp.dma_start(tile[0:P - 1, :], edge_rows(a, o)).then_inc(tables_in, 16)
                sp.dma_start(tile[P - 1:P, 0:REST_E - o],
                             a[FULL_E + o:E].rearrange("(p t) -> p t", p=1)).then_inc(tables_in, 16)
            sp.dma_start(next_last[0:P - 2, :], edge_rows(dst)[1:P - 1, ET - 1:ET],
                         allow_slow_non_contiguous=True).then_inc(tables_in, 16)
            sp.dma_start(after_next[0:P - 2, :], dst[ET + 1:ET + 1 + (P - 2) * ET]
                         .rearrange("(p t) -> p t", t=ET)[:, ET - 1:ET],
                         allow_slow_non_contiguous=True).then_inc(tables_in, 16)

            sp.wait_ge(fill_ready, 2)

            def load_x(i, s, rows, tiles):
                after(sp, x_used[s], i)
                sp.dma_start(work[s][0:rows, 0:tiles * D], node_rows(x, i, s, rows, tiles)).then_inc(x_in[s], 16)
                sp.dma_start(node_rows(gat_d, i, s, rows, tiles), work[12][0:rows, 0:tiles * ROW]).then_inc(filled, 16)
            node_groups(sp, load_x)
            sp.wait_ge(filled, 16 * (NG + 1))
            end_stage(sp, 1)

            def fill_zero(i, s, rows, tiles):
                sp.dma_start(node_rows(agg_d, i, s, rows, tiles), work[13][0:rows, 0:tiles * D]).then_inc(filled, 16)
            node_groups(sp, fill_zero)
            sp.wait_ge(filled, 32 * (NG + 1))
            end_stage(sp, 2)

            def load_ag(i, s, rows, tiles):
                after(sp, ag_used[s], i)
                sp.dma_start(work[s][0:rows, 0:tiles * ROW], node_rows(gat_d, i, s, rows, tiles)).then_inc(ag_in[s], 16)
                sp.dma_start(work[2 + s][0:rows, 0:tiles * D], node_rows(xl_d, i, s, rows, tiles)).then_inc(ag_in[s], 16)
            node_groups(sp, load_ag)
            end_stage(sp, 3)

            def load_nx(i, s, rows, tiles):
                after(sp, nx_used[s], i)
                sp.dma_start(work[s][0:rows, 0:tiles * D], node_rows(conv_d, i, s, rows, tiles)).then_inc(nx_in[s], 16)
                sp.dma_start(work[2 + s][0:rows, 0:tiles * D], node_rows(x, i, s, rows, tiles)).then_inc(nx_in[s], 16)
            node_groups(sp, load_nx)
            end_stage(sp, 4)

            for l in range(LAYERS):
                r = rel[l]
                end_stage(sp, 5 + 2 * l)
                h_d = (x1_d, h1_d)[l]

                def load_n(i, s, rows, tiles):
                    after(sp, r["s_ok" if l == 0 else "z_ok"][s], i)
                    parts = [(0, agg_d), (2, h_d)] + ([(4, x1_d)] if l == LAYERS - 1 else [])
                    for k, d in parts:
                        sp.dma_start(work[k + s][0:rows, 0:tiles * D],
                                     node_rows(d, i, s, rows, tiles)).then_inc(r["n_in"][s], 16)
                node_groups(sp, load_n)
                end_stage(sp, 6 + 2 * l)

        @block.gpsimd
        def _(pool):
            st = Steps(pool, pool_steps)
            pool.iota(rel_id[:, :], [[1, RELS]], base=0, channel_multiplier=0,
                      allow_small_or_imprecise_dtypes=True).then_inc(consts, 1)
            st.did(pool.memset(ident[:, :], 0.0))
            st.wait()
            pool.affine_select(out=ident[:, :], in_=ident[:, :], compare_op=ALU.not_equal, fill=1.0,
                               base=0, pattern=[[-1, P]], channel_multiplier=1).then_inc(consts, 1)
            pool.memset(ones[:, :], 1.0).then_inc(consts, 1)

            def store(dram, k, done, i, s, rows, tiles):
                pool.dma_start(node_rows(dram, i, s, rows, tiles), work[k + s][0:rows, 0:tiles * D]).then_inc(done[s], 16)

            def store_lr(i, s, rows, tiles):
                wait_group(pool, r_cp, i, s, tiles)
                wait_group(pool, l_cp, i, s, tiles)
                alone(pool)
                for k, dram in enumerate((xl_d, xr_d)):
                    pool.dma_start(node_rows(dram, i, s, rows, tiles).rearrange("p (t d) -> p t d", d=D),
                                   lr[0:rows, s, 0:tiles, k * D:(k + 1) * D]).then_inc(lr_out[s], 16)
            node_groups(pool, store_lr)
            pool.wait_ge(lr_out[0], 32 * (LAST + 1))
            pool.wait_ge(lr_out[1], 32 * LAST)
            pool.wait_ge(tables_ok, 1)
            end_stage(pool, 1)

            def gather_at(i, s):
                after(pool, at_row[s], i)
                after(pool, at_out[s], 16 * EG * i)
                alone(pool)
                for k, table in enumerate((src_i, xr_idx, out_idx)):
                    st.did(pool.tensor_copy(idx_st[:, s, k, :], table[:, bass.ds((2 * i + s) * EG, EG)]))
                st.wait()
                alone(pool)
                for t in range(EG):
                    pool.indirect_dma_start(tiles_of(s)[:, t, :], None, xl_d,
                                            bass.IndirectOffsetOnAxis(ap=idx_st[:, s, 0, t:t + 1], axis=0)).then_inc(at_in[s], 16)
                    pool.indirect_dma_start(tiles_of(2 + s)[:, t, :], None, xr_d,
                                            bass.IndirectOffsetOnAxis(ap=idx_st[:, s, 1, t:t + 1], axis=0)).then_inc(at_in[s], 16)

            def scatter_at(i, s):
                pool.wait_ge(at_row[s], i + 1)
                alone(pool)
                for t in range(EG):
                    pool.indirect_dma_start(gat_d, bass.IndirectOffsetOnAxis(ap=idx_st[:, s, 2, t:t + 1], axis=0),
                                            tiles_of(4 + s, EG, ROW)[:, t, :], None,
                                            bounds_check=N - 1, oob_is_err=False).then_inc(at_out[s], 16)

            def exchange_at(i):
                gather_at(i, 1)
                scatter_at(i, 0)
                gather_at(i + 1, 0)
                scatter_at(i, 1)
            gather_at(0, 0)
            in_pairs(pool, exchange_at, EITER - 1, st)
            gather_at(EITER - 1, 1)
            scatter_at(EITER - 1, 0)
            scatter_at(EITER - 1, 1)
            for s in range(2):
                pool.wait_ge(at_out[s], 16 * EG * EITER)
            by_fix = bass.IndirectOffsetOnAxis(ap=fix_idx[:, 0:1], axis=0)
            pool.wait_ge(fixed, 1)
            pool.indirect_dma_start(fix[:, 0, :], None, gat_d, by_fix, bounds_check=N - 1, oob_is_err=False).then_inc(fix_in, 16)
            pool.wait_ge(fixed, 2)
            pool.indirect_dma_start(gat_d, by_fix, fix[:, 1, :], None, bounds_check=N - 1, oob_is_err=False).then_inc(fix_out, 16)
            pool.wait_ge(fix_out, 16)
            end_stage(pool, 2)

            def store_cv(i, s, rows, tiles):
                pool.wait_ge(cv_ok[s], i + 1)
                alone(pool)
                store(conv_d, 4, cv_out, i, s, rows, tiles)
            node_groups(pool, store_cv)
            pool.wait_ge(cv_out[0], 16 * (LAST + 1))
            pool.wait_ge(cv_out[1], 16 * LAST)
            end_stage(pool, 3)

            def store_nx(i, s, rows, tiles):
                pool.wait_ge(nx_ok[s], i + 1)
                alone(pool)
                store(x1_d, 4, nx_out, i, s, rows, tiles)
            node_groups(pool, store_nx)
            pool.wait_ge(nx_out[0], 16 * (LAST + 1))
            pool.wait_ge(nx_out[1], 16 * LAST)
            end_stage(pool, 4)

            for l in range(LAYERS):
                r = rel[l]
                h_d = (x1_d, h1_d)[l]

                def gather_h(i, s):
                    after(pool, r["row"][s], i)
                    after(pool, r["out"][s], 16 * EG * i)
                    alone(pool)
                    for k, table in ((0, src_i), (2, out_idx)):
                        st.did(pool.tensor_copy(idx_st[:, s, k, :], table[:, bass.ds((2 * i + s) * EG, EG)]))
                    st.wait()
                    alone(pool)
                    for t in range(EG):
                        pool.indirect_dma_start(tiles_of(s)[:, t, :], None, h_d,
                                                bass.IndirectOffsetOnAxis(ap=idx_st[:, s, 0, t:t + 1], axis=0)).then_inc(r["h_in"][s], 16)

                def scatter_h(i, s):
                    pool.wait_ge(r["row"][s], i + 1)
                    alone(pool)
                    for t in range(EG):
                        pool.indirect_dma_start(agg_d, bass.IndirectOffsetOnAxis(ap=idx_st[:, s, 2, t:t + 1], axis=0),
                                                tiles_of(4 + s)[:, t, :], None,
                                                bounds_check=N - 1, oob_is_err=False).then_inc(r["out"][s], 16)

                def exchange_h(i):
                    gather_h(i, 1)
                    scatter_h(i, 0)
                    gather_h(i + 1, 0)
                    scatter_h(i, 1)
                gather_h(0, 0)
                in_pairs(pool, exchange_h, EITER - 1, st)
                gather_h(EITER - 1, 1)
                scatter_h(EITER - 1, 0)
                scatter_h(EITER - 1, 1)
                for s in range(2):
                    pool.wait_ge(r["out"][s], 16 * EG * EITER)
                pool.indirect_dma_start(fix[:, 0, 0:D], None, agg_d, by_fix, bounds_check=N - 1, oob_is_err=False).then_inc(r["fix_in"], 16)
                pool.wait_ge(r["fix_row"], 1)
                pool.indirect_dma_start(agg_d, by_fix, fix[:, 1, 0:D], None, bounds_check=N - 1, oob_is_err=False).then_inc(r["fix_out"], 16)
                pool.wait_ge(r["fix_out"], 16)
                end_stage(pool, 5 + 2 * l)

                def store_h(i, s, rows, tiles):
                    pool.wait_ge(r["nh_ok"][s], i + 1)
                    alone(pool)
                    store((h1_d, out)[l], 6, r["nh_out"], i, s, rows, tiles)
                node_groups(pool, store_h)
                pool.wait_ge(r["nh_out"][0], 16 * (LAST + 1))
                pool.wait_ge(r["nh_out"][1], 16 * LAST)
                end_stage(pool, 6 + 2 * l)

        @block.tensor
        def _(pe):
            pe.wait_ge(consts, 3)
            pe.wait_ge(weights_in, 16 * 11)

            def transpose_chunk(tiles, rows, c, t0, n, use, ps, cp):
                after(pe, cp[c % 2], use)
                for t in range(t0, t0 + n):
                    last = pe.transpose(psum[c % 2][:, (t - t0) * P:(t - t0) * P + rows],
                                        tiles[0:rows, t, :], ident[0:rows, 0:rows])
                last.then_inc(ps[c % 2], 1)

            def project(i, s, rows, tiles):
                pe.wait_ge(x_in[s], 16 * (i + 1))
                todo = chunks(tiles)

                def multiply(c, t0, n):
                    use = 4 * i + 2 * s + c // 2
                    b = c % 2
                    pe.wait_ge(xt_cp[b], use + 1)
                    after(pe, l_cp[b], use)
                    after(pe, r_cp[b], use)
                    for t in range(t0, t0 + n):
                        k = t - t0
                        last = pe.matmul(psum[2 + 2 * b + k // 2][0:rows, (k % 2) * 256:(k % 2) * 256 + 256],
                                         tiles_of(8 + s)[:, t, 0:rows], w_lr[:, :], start=True, stop=True)
                        if c == len(todo) - 2 and k == 0:
                            last.then_inc(x_used[s], 1)
                    last.then_inc(lr_ps[b], 1)

                for c, t0, n in todo:
                    transpose_chunk(tiles_of(s), rows, c, t0, n, 4 * i + 2 * s + c // 2, xt_ps, xt_cp)
                    if c:
                        multiply(*todo[c - 1])
                multiply(*todo[-1])
            node_groups(pe, project)
            end_stage(pe, 1)

            pe.wait_ge(fix_rd, 1)
            pe.matmul(psum[0][:, 0:P], ones[:, :], edge_m[:, 0, :], start=True, stop=True)
            pe.matmul(psum[0][:, P:2 * P], ones[:, :], edge_m[:, 1, :], start=True, stop=True)
            pe.matmul(psum[1][:, :], ones[:, :], diag[:, :, :].rearrange("p h q -> p (h q)"), start=True, stop=True).then_inc(fix_mm, 1)
            pe.wait_ge(fix_rd, 3)
            pe.matmul(psum[2][:, 0:D + H], edge_m[:, 0, :], work[10][:, 0:D + H], start=True, stop=True).then_inc(fix_mm, 1)
            end_stage(pe, 2)

            pe.wait_ge(zeroed, 1)
            for b in range(2):
                pe.matmul(psum[b][:, :], ones[:, :], work[12][:, 0:512], start=True, stop=False, skip_group_check=True)

            def sums(i, s, rows, tiles):
                for b, (sig, k) in enumerate(((cv_ok, 4), (cv_sq, 6))):
                    pe.wait_ge(sig[s], i + 1)
                    for c, t0, n in chunks(tiles):
                        last = pe.matmul(psum[b][:, 0:n * D], ones[0:rows, :],
                                         work[k + s][0:rows, t0 * D:(t0 + n) * D], start=False, stop=False,
                                         skip_group_check=True)
                last.then_inc(cv_mm[s], 1)
            node_groups(pe, sums)
            end_stage(pe, 3)
            end_stage(pe, 4)

            for l in range(LAYERS):
                r = rel[l]

                def edge_tiles(i, s):
                    pe.wait_ge(r["h_in"][s], 16 * EG * (i + 1))
                    parts = [(0, 0, 4), (1, 4, EG - 4)]

                    def expand(c, t0, n):
                        pe.wait_ge(r["t_cp"][c], 2 * i + s + 1)
                        for t in range(t0, t0 + n):
                            k = s * EG + t
                            after(pe, r["y_used"][k % 2], EG * i + k // 2)
                            pe.matmul(psum[2 + k % 2][:, :], tiles_of(2 + s)[:, t, :],
                                      basis_s[:, l, :, :].rearrange("k b n -> k (b n)"), start=True, stop=True).then_inc(r["y_ps"][k % 2], 1)
                    for c, t0, n in parts:
                        after(pe, r["t_cp"][c], 2 * i + s)
                        for t in range(t0, t0 + n):
                            last = pe.transpose(psum[c][:, (t - t0) * P:(t - t0 + 1) * P], tiles_of(s)[:, t, :], ident[:, :])
                        last.then_inc(r["t_ps"][c], 1)
                    for part in parts:
                        expand(*part)
                def edge_pair(i):
                    edge_tiles(i, 0)
                    edge_tiles(i, 1)
                in_pairs(pe, edge_pair, EITER)
                pe.wait_ge(r["row"][1], EITER)
                pe.matmul(psum[0][:, 0:D], edge_m[:, 0, :], tiles_of(5)[:, EG - 1, :], start=True, stop=True).then_inc(r["fix_mm"], 1)
                end_stage(pe, 5 + 2 * l)

                def nodes(i, s, rows, tiles):
                    pe.wait_ge(r["n_in"][s], (32 + 16 * l) * (i + 1))
                    todo = chunks(tiles)

                    def multiply(c, t0, n):
                        use, b = 4 * i + 2 * s + c // 2, c % 2
                        pe.wait_ge(r["nt_cp"][b], use + 1)
                        after(pe, r["nm_used"][b], use)
                        for t in range(t0, t0 + n):
                            last = pe.matmul(psum[2 + b][0:rows, (t - t0) * D:(t - t0 + 1) * D],
                                             tiles_of(8 + s)[:, t, 0:rows], loop_s[:, l, :], start=True, stop=True)
                        last.then_inc(r["nm_ps"][b], 1)

                    for c, t0, n in todo:
                        transpose_chunk(tiles_of(2 + s), rows, c, t0, n, 4 * i + 2 * s + c // 2, r["nt_ps"], r["nt_cp"])
                        if c:
                            multiply(*todo[c - 1])
                    multiply(*todo[-1])
                node_groups(pe, nodes)
                end_stage(pe, 6 + 2 * l)

        @block.scalar
        def _(act):
            st = Steps(act, act_steps)

            def copy_turned(i, s, rows, n, c, t0, k, ps, cp):
                act.wait_ge(ps[c % 2], 4 * i + 2 * s + c // 2 + 1)
                act.activation(tiles_of(k + s)[:, t0:t0 + n, 0:rows],
                               psum[c % 2][:, 0:n * P].rearrange("p (t d) -> p t d", d=P)[:, :, 0:rows],
                               ACT.Copy).then_inc(cp[c % 2], 1)

            def project(i, s, rows, tiles):
                todo = chunks(tiles)
                after(act, lr_out[s], 32 * i)
                after(act, l_read[s], i)

                def copy_l(c, t0, n):
                    b, m = c % 2, min(2, n)
                    act.wait_ge(lr_ps[b], 4 * i + 2 * s + c // 2 + 1)
                    act.activation(lr[0:rows, s, t0:t0 + m, :].rearrange("p t d -> p (t d)"),
                                   psum[2 + 2 * b][0:rows, 0:m * 256], ACT.Copy).then_inc(l_cp[b], 1)
                for c, t0, n in todo:
                    copy_turned(i, s, rows, n, c, t0, 8, xt_ps, xt_cp)
                    if c:
                        copy_l(*todo[c - 1])
                copy_l(*todo[-1])
            node_groups(act, project)
            end_stage(act, 1)

            with act.Fori(0, EGROUPS) as g:
                act.wait_ge(at_arg, g + 1)
                act.activation(exp_out[:, :, :, :], exp_in[:, :, :, :], ACT.Exp).then_inc(at_exp, 1)
            act.wait_ge(fix_rd, 2)
            act.activation(fix_s[:, 2, :], fix_s[:, 1, :], ACT.Exp).then_inc(fix_act, 1)
            act.wait_ge(fix_rd, 4)
            act.activation(fix_s[:, 6:8, :], fix_s[:, 4:6, :], ACT.Exp).then_inc(fix_act, 1)
            end_stage(act, 2)

            def exps(i, s, rows, tiles):
                act.wait_ge(ag_arg, 2 * i + s + 1)
                act.activation(nexp_out[0:rows, :, 0:tiles, :], nexp_in[0:rows, :, 0:tiles, :], ACT.Exp).then_inc(ag_exp, 1)
                act.wait_ge(cv_ok[s], i + 1)
                after(act, cv_mm[s], i)
                act.activation(work[6 + s][0:rows, 0:tiles * D], work[4 + s][0:rows, 0:tiles * D], ACT.Square).then_inc(cv_sq[s], 1)
            node_groups(act, exps)
            act.wait_ge(gn_var, 1)
            act.activation(stat[:, 5, :], stat[:, 4, :], ACT.Sqrt).then_inc(gn_std, 1)
            end_stage(act, 3)

            def elus(i, s, rows, tiles):
                act.wait_ge(nx_y, 2 * i + s + 1)
                w = tiles * D
                st.did(act.activation(work[8][0:rows, 0:w], work[6][0:rows, 0:w], ACT.Relu, scale=-1.0))
                st.wait()
                act.activation(work[7][0:rows, 0:w], work[8][0:rows, 0:w], ACT.Exp, scale=-1.0).then_inc(nx_e, 1)
                act.wait_ge(nx_v, 2 * i + s + 1)
                act.activation(rstd[0:rows, 1, 0:tiles], rstd[0:rows, 0, 0:tiles], ACT.Sqrt).then_inc(nx_r, 1)
            node_groups(act, elus, st)
            end_stage(act, 4)

            for l in range(LAYERS):
                r = rel[l]

                def turned(i, s):
                    for c, t0, n in ((0, 0, 4), (1, 4, EG - 4)):
                        act.wait_ge(r["t_ps"][c], 2 * i + s + 1)
                        act.activation(tiles_of(2 + s)[:, t0:t0 + n, :],
                                       psum[c][:, 0:n * P].rearrange("p (t d) -> p t d", d=P),
                                       ACT.Copy).then_inc(r["t_cp"][c], 1)
                def turned_pair(i):
                    turned(i, 0)
                    turned(i, 1)
                in_pairs(act, turned_pair, EITER)
                end_stage(act, 5 + 2 * l)

                def nodes(i, s, rows, tiles):
                    for c, t0, n in chunks(tiles):
                        copy_turned(i, s, rows, n, c, t0, 8, r["nt_ps"], r["nt_cp"])
                    act.wait_ge(r["s_ok"][s], i + 1)
                    if l == 0:
                        after(act, r["nh_out"][s], 16 * i)
                        to, done = work[6 + s], r["nh_ok"]
                    else:
                        after(act, r["nh_ok"][s], i)
                        to, done = work[12 + s], r["h_ok"]
                    act.activation(to[0:rows, 0:tiles * D], work[10 + s][0:rows, 0:tiles * D], ACT.Tanh).then_inc(done[s], 1)
                    if l == LAYERS - 1:
                        act.wait_ge(r["v_ok"], 2 * i + s + 1)
                        act.activation(rstd[0:rows, 1, 0:tiles], rstd[0:rows, 0, 0:tiles], ACT.Sqrt).then_inc(r["r_ok"], 1)
                node_groups(act, nodes)
                end_stage(act, 6 + 2 * l)

        @block.vector
        def _(dve):
            st = Steps(dve, dve_steps)

            def over_tiles(row, rows, tiles):
                return row.unsqueeze(1).to_broadcast([rows, tiles, D])

            def per_head(small):
                a = small.unsqueeze(len(small.shape))
                return a.to_broadcast(list(small.shape) + [C])

            for tile, v in ((src_i, 0), (dst_i, PAD_DST), (next_i, FAR), (etype_i, 0), (next_last, FAR), (after_next, FAR + 1)):
                dve.memset(tile[:, :], v).then_inc(cleared, 1)
            st.did(dve.memset(work[12][:, :], 0.0))
            dve.memset(work[13][:, :], 0.0).then_inc(fill_ready, 1)
            st.wait()
            dve.memset(tiles_of(12, NT, ROW)[:, :, D + H:ROW], -LOW).then_inc(fill_ready, 1)

            dve.wait_ge(tables_in, 16 * 10)
            st.did(dve.memset(cont[:, 0:1], 0.0))
            st.did(dve.tensor_tensor(cont[:, 1:ET], dst_i[:, 1:ET], dst_i[:, 0:ET - 1], ALU.is_equal))
            st.did(dve.tensor_scalar(xr_idx[:, :], dst_i[:, :], N - 1.0, None, ALU.min))
            st.did(dve.tensor_tensor(drop[:, :], dst_i[:, :], next_i[:, :], ALU.is_equal))
            st.did(dve.tensor_copy(last_f[:, :], dst_i[:, ET - 1:ET]))
            st.wait()
            st.did(dve.tensor_copy(flag[:, 0:1], drop[:, ET - 1:ET]))
            st.did(dve.scalar_tensor_tensor(out_idx[:, :], drop[:, :], float(FAR), dst_i[:, :], ALU.mult, ALU.add))
            st.did(dve.tensor_tensor(flag[:, 1:2], next_last[:, :], dst_i[:, ET - 1:ET], ALU.is_equal))
            st.did(dve.tensor_tensor(flag[:, 2:3], next_last[:, :], after_next[:, :], ALU.is_equal))
            st.wait()
            st.did(dve.tensor_scalar(drop[:, :], cont[:, :], 1.0, LOW, ALU.subtract, ALU.mult))
            st.did(dve.tensor_tensor(flag[:, 1:2], flag[:, 1:2], flag[:, 2:3], ALU.mult))
            st.wait()
            st.did(dve.tensor_scalar(flag[:, 2:3], flag[:, 1:2], -1.0, 1.0, ALU.mult, ALU.add))
            st.wait()
            st.did(dve.tensor_tensor(flag[:, 3:4], flag[:, 0:1], flag[:, 2:3], ALU.mult))
            st.wait()
            st.did(dve.tensor_scalar(flag[:, 2:3], flag[:, 3:4], -float(FAR), float(FAR), ALU.mult, ALU.add))
            st.wait()
            dve.tensor_tensor(fix_idx[:, :], flag[:, 2:3], last_f[:, :], ALU.add).then_inc(tables_ok, 1)

            dve.wait_ge(weights_in, 16 * 11)

            def project(i, s, rows, tiles):
                after(dve, lr_out[s], 32 * i)
                for c, t0, n in chunks(tiles):
                    b = c % 2
                    dve.wait_ge(lr_ps[b], 4 * i + 2 * s + c // 2 + 1)
                    if n > 2:
                        dve.tensor_copy(lr[0:rows, s, t0 + 2:t0 + n, :].rearrange("p t d -> p (t d)"),
                                        psum[3 + 2 * b][0:rows, 0:(n - 2) * 256]).then_inc(r_cp[b], 1)
                    else:
                        dve.sem_inc(r_cp[b], 1)
                wait_group(dve, l_cp, i, s, tiles)
                wait_group(dve, r_cp, i, s, tiles)
                after(dve, l_read[1 - s], i + s)
                m_t = tiles_of(10)[0:rows, 0:tiles, :]
                st.did(dve.tensor_tensor(m_t, lr[0:rows, s, 0:tiles, 0:D], lr[0:rows, s, 0:tiles, D:2 * D], ALU.add))
                st.wait()
                st.did(dve.scalar_tensor_tensor(m_t, m_t, SLOPE, m_t, ALU.mult, ALU.max))
                st.wait()
                st.did(dve.tensor_tensor(m_t, m_t, over_tiles(att_b[0:rows, :], rows, tiles), ALU.mult))
                st.wait()
                at = bass.ds((2 * i + s) * NT, NT) if rows == P else slice(NG * NT, NG * NT + 1)
                dve.tensor_reduce(self_logit[0:rows, at, :], m_t.rearrange("p t (h c) -> p t h c", h=H),
                                  AX.X, ALU.add).then_inc(l_read[s], 1)
            node_groups(dve, project, st)
            end_stage(dve, 1)

            rows_of = lambda s: tiles_of(4 + s, EG, ROW)
            st.did(dve.memset(rows_of(1)[:, EG - 1, :], 0.0))
            st.wait()

            def attend(i, s):
                dve.wait_ge(at_in[s], 32 * EG * (i + 1))
                xs = tiles_of(s)[:, 0:EG, :]
                tmp = tiles_of(8)[:, 0:EG, :]
                R, before = rows_of(s), rows_of(1 - s)
                after(dve, at_row[1 - s], i + s)
                st.did(dve.tensor_tensor(tmp, xs, tiles_of(2 + s)[:, 0:EG, :], ALU.add))
                st.did(dve.tensor_copy(drop_st[:, s, :], drop[:, bass.ds((2 * i + s) * EG, EG)]))
                st.wait()
                st.did(dve.scalar_tensor_tensor(tmp, tmp, SLOPE, tmp, ALU.mult, ALU.max))
                st.wait()
                st.did(dve.tensor_tensor(tmp, tmp, over_tiles(att_b[:, :], P, EG), ALU.mult))
                st.wait()
                st.did(dve.tensor_reduce(logit[:, :, :], tmp.rearrange("p t (h c) -> p t h c", h=H), AX.X, ALU.add))
                st.wait()
                after(dve, at_out[s], 16 * EG * i)
                for h in range(H):
                    st.did(dve.tensor_tensor_scan(R[:, :, D + H + h], drop_st[:, s, :], logit[:, :, h],
                                                  before[:, EG - 1, D + H + h:D + H + h + 1], ALU.add, ALU.max))
                st.wait()
                mx = R[:, :, D + H:ROW]
                st.did(dve.tensor_tensor(exp_in[:, 0, 0, :], before[:, EG - 1, D + H:ROW], mx[:, 0, :], ALU.subtract))
                st.did(dve.tensor_tensor(exp_in[:, 0, 1:EG, :], mx[:, 0:EG - 1, :], mx[:, 1:EG, :], ALU.subtract))
                st.did(dve.tensor_tensor(exp_in[:, 1, :, :], logit[:, :, :], mx, ALU.subtract))
                st.wait()
                dve.tensor_tensor(exp_in[:, 0, :, :], exp_in[:, 0, :, :],
                                  drop_st[:, s, :].unsqueeze(2).to_broadcast([P, EG, H]), ALU.add).then_inc(at_arg, 1)
                dve.wait_ge(at_exp, 2 * i + s + 1)
                fade, gain = exp_out[:, 0, :, :], exp_out[:, 1, :, :]
                val = tiles_of(9)[:, 0:EG, :]
                st.did(dve.tensor_tensor(val.rearrange("p t (h c) -> p t h c", h=H), xs.rearrange("p t (h c) -> p t h c", h=H),
                                         per_head(gain), ALU.mult))
                for h in range(H):
                    st.did(dve.tensor_tensor_scan(R[:, :, D + h], fade[:, :, h], gain[:, :, h],
                                                  before[:, EG - 1, D + h:D + h + 1], ALU.mult, ALU.add))
                st.wait()
                carried = work[10][:, 0:D]
                for t in range(EG):
                    prev = R[:, t - 1, 0:D] if t else before[:, EG - 1, 0:D]
                    st.did(dve.tensor_tensor(carried.rearrange("p (h c) -> p h c", h=H), prev.rearrange("p (h c) -> p h c", h=H),
                                             per_head(fade[:, t, :]), ALU.mult))
                    st.wait()
                    ins = dve.tensor_tensor(R[:, t, 0:D], carried, val[:, t, :], ALU.add)
                    if t < EG - 1:
                        st.did(ins)
                        st.wait()
                ins.then_inc(at_row[s], 1)

            def coefficients(i, s):
                at = bass.ds((2 * i + s) * EG, EG)
                hot = work[11][:, 0:EG * RELS].rearrange("p (t r) -> p t r", r=RELS)
                prod = work[11][:, EG * RELS:EG * RELS * (1 + BASES)].rearrange("p (t b r) -> p t b r", b=BASES, r=RELS)
                st.did(dve.tensor_tensor(hot, etype_i[:, at].unsqueeze(2).to_broadcast([P, EG, RELS]),
                                         rel_id[:, :].unsqueeze(1).to_broadcast([P, EG, RELS]), ALU.is_equal))
                st.wait()
                for l in range(LAYERS):
                    for b in range(BASES):
                        st.did(dve.tensor_tensor(prod[:, :, b, :], hot,
                                                 comp_b[:, l, :, b].unsqueeze(1).to_broadcast([P, EG, RELS]), ALU.mult))
                    st.wait()
                    st.did(dve.tensor_reduce(coef[:, l, at, :], prod, AX.X, ALU.add))
                    st.wait()

            def attend_pair(i):
                for s in range(2):
                    attend(i, s)
                    coefficients(i, s)
            in_pairs(dve, attend_pair, EITER, st)

            open_row = rows_of(1)[:, EG - 1, :]
            dve.wait_ge(at_row[1], EITER)
            dve.tensor_scalar(edge_m[:, 0, :], ident[:, :], last_f[:, 0:1], None, ALU.mult)
            dve.tensor_scalar(edge_m[:, 1, :], ident[:, :], flag[:, 0:1], None, ALU.mult)
            for h in range(H):
                last = dve.tensor_scalar(diag[:, h, :], ident[:, :], open_row[:, D + H + h:D + H + h + 1], None, ALU.mult)
            last.then_inc(fix_rd, 1)
            dve.memset(fix[:, :, :], 0.0).then_inc(fixed, 1)
            dve.wait_ge(fix_mm, 1)
            st.did(dve.tensor_scalar(edge_m[:, 2, :], psum[0][:, 0:P], last_f[:, 0:1], None, ALU.is_equal))
            st.wait()
            st.did(dve.tensor_scalar(edge_m[:, 0, :], edge_m[:, 2, :], flag[:, 0:1], None, ALU.mult))
            st.did(dve.tensor_tensor(edge_m[:, 2, :], edge_m[:, 2, :], psum[0][:, P:2 * P], ALU.mult))
            st.wait()
            st.did(dve.tensor_scalar(edge_m[:, 2, :], edge_m[:, 2, :], 1.0, LOW, ALU.subtract, ALU.mult))
            st.wait()
            st.did(dve.tensor_tensor(diag[:, :, :], psum[1][:, :].rearrange("p (h q) -> p h q", h=H),
                                     edge_m[:, 2, :].unsqueeze(1).to_broadcast([P, H, P]), ALU.add))
            st.wait()
            st.did(dve.tensor_reduce(fix_s[:, 0, :], diag[:, :, :], AX.X, ALU.max))
            st.wait()
            st.did(dve.tensor_tensor(fix_s[:, 1, :], open_row[:, D + H:ROW], fix_s[:, 0, :], ALU.subtract))
            st.wait()
            dve.tensor_scalar(fix_s[:, 1, :], fix_s[:, 1, :], 0.0, None, ALU.min).then_inc(fix_rd, 1)
            heads = lambda a: a.rearrange("p (h c) -> p h c", h=H)
            dve.wait_ge(fix_act, 1)
            dve.tensor_tensor(heads(work[10][:, 0:D]), heads(open_row[:, 0:D]), per_head(fix_s[:, 2, :]), ALU.mult)
            dve.tensor_tensor(work[10][:, D:D + H], open_row[:, D:D + H], fix_s[:, 2, :], ALU.mult).then_inc(fix_rd, 1)
            dve.wait_ge(fix_in, 16)
            st.did(dve.tensor_tensor(fix_s[:, 3, :], fix[:, 0, D + H:ROW], fix_s[:, 0, :], ALU.max))
            st.wait()
            dve.tensor_tensor(fix_s[:, 4, :], fix[:, 0, D + H:ROW], fix_s[:, 3, :], ALU.subtract)
            dve.tensor_tensor(fix_s[:, 5, :], fix_s[:, 0, :], fix_s[:, 3, :], ALU.subtract).then_inc(fix_rd, 1)
            dve.wait_ge(fix_act, 2)
            dve.wait_ge(fix_mm, 2)
            st.did(dve.tensor_tensor(heads(fix[:, 0, 0:D]), heads(fix[:, 0, 0:D]), per_head(fix_s[:, 6, :]), ALU.mult))
            st.did(dve.tensor_tensor(fix[:, 0, D:D + H], fix[:, 0, D:D + H], fix_s[:, 6, :], ALU.mult))
            st.did(dve.tensor_tensor(heads(fix[:, 1, 0:D]), heads(psum[2][:, 0:D]), per_head(fix_s[:, 7, :]), ALU.mult))
            st.did(dve.tensor_tensor(fix[:, 1, D:D + H], psum[2][:, D:D + H], fix_s[:, 7, :], ALU.mult))
            st.did(dve.tensor_copy(fix[:, 1, D + H:ROW], fix_s[:, 3, :]))
            st.wait()
            dve.tensor_tensor(fix[:, 1, 0:D + H], fix[:, 1, 0:D + H], fix[:, 0, 0:D + H], ALU.add).then_inc(fixed, 1)
            end_stage(dve, 2)

            dve.memset(work[12][:, 0:512], 0.0).then_inc(zeroed, 1)

            def merge(i, s, rows, tiles):
                at = bass.ds((2 * i + s) * NT, NT) if rows == P else slice(NG * NT, NG * NT + 1)
                dve.wait_ge(ag_in[s], 32 * (i + 1))
                row = tiles_of(s, NT, ROW)[0:rows, 0:tiles, :]
                own = self_logit[0:rows, at, :]
                mx, den, tmp = (nsm[0:rows, k, 0:tiles, :] for k in range(3))
                e_in, e_out = nexp_in[0:rows, :, 0:tiles, :], nexp_out[0:rows, :, 0:tiles, :]
                st.did(dve.tensor_tensor(mx, row[:, :, D + H:ROW], own, ALU.max))
                st.wait()
                dve.tensor_tensor(e_in[:, 0], row[:, :, D + H:ROW], mx, ALU.subtract)
                dve.tensor_tensor(e_in[:, 1], own, mx, ALU.subtract).then_inc(ag_arg, 1)
                dve.wait_ge(ag_exp, 2 * i + s + 1)
                st.did(dve.tensor_tensor(den, row[:, :, D:D + H], e_out[:, 0], ALU.mult))
                st.wait()
                st.did(dve.scalar_tensor_tensor(den, den, 1e-16, e_out[:, 1], ALU.add, ALU.add))
                st.wait()
                st.did(dve.reciprocal(tmp, den))
                st.wait()
                for k in range(2):
                    st.did(dve.tensor_tensor(e_out[:, k], e_out[:, k], tmp, ALU.mult))
                st.wait()
                split = lambda a: a.rearrange("p t (h c) -> p t h c", h=H)
                part, own_part = tiles_of(9)[0:rows, 0:tiles, :], tiles_of(8)[0:rows, 0:tiles, :]
                st.did(dve.tensor_tensor(split(part), split(row[:, :, 0:D]), per_head(e_out[:, 0]), ALU.mult))
                dve.tensor_tensor(split(own_part), split(tiles_of(2 + s)[0:rows, 0:tiles, :]), per_head(e_out[:, 1]),
                                  ALU.mult).then_inc(ag_used[s], 1)
                st.wait()
                dve.wait_ge(ag_used[s], i + 1)
                after(dve, cv_out[s], 16 * i)
                after(dve, cv_mm[s], i)
                dve.tensor_tensor(tiles_of(4 + s)[0:rows, 0:tiles, :], part, own_part, ALU.add).then_inc(cv_ok[s], 1)
            node_groups(dve, merge, st)

            dve.wait_ge(cv_mm[0], LAST + 1)
            dve.wait_ge(cv_mm[1], LAST)
            for b in range(2):
                st.did(dve.tensor_reduce(stat[:, b, :], psum[b][:, :].rearrange("p (k d) -> p d k", d=D), AX.X, ALU.add))
            st.wait()
            mean, sq, k_, d2, var = (stat[:, k, :] for k in range(5))
            st.did(dve.tensor_scalar(stat[:, 0:2, :], stat[:, 0:2, :], 1.0 / N, None, ALU.mult))
            st.wait()
            st.did(dve.tensor_tensor(k_, mean, conv_b[:, :], ALU.add))
            st.did(dve.tensor_tensor(d2, mean, mean, ALU.mult))
            st.wait()
            st.did(dve.tensor_tensor(k_, k_, gms_b[:, :], ALU.mult))
            st.did(dve.tensor_tensor(sq, sq, d2, ALU.subtract))
            st.wait()
            st.did(dve.tensor_tensor(k_, k_, conv_b[:, :], ALU.subtract))
            st.did(dve.tensor_scalar(sq, sq, 0.0, None, ALU.max))
            st.wait()
            st.did(dve.tensor_tensor(d2, mean, k_, ALU.subtract))
            st.wait()
            st.did(dve.tensor_tensor(d2, d2, d2, ALU.mult))
            st.wait()
            dve.scalar_tensor_tensor(var, d2, EPS, sq, ALU.add, ALU.add).then_inc(gn_var, 1)
            dve.wait_ge(gn_std, 1)
            st.did(dve.reciprocal(var, stat[:, 5, :]))
            st.wait()
            st.did(dve.tensor_tensor(gn_scale[:, :], var, gnw_b[:, :], ALU.mult))
            st.wait()
            st.did(dve.tensor_tensor(d2, k_, gn_scale[:, :], ALU.mult))
            st.wait()
            dve.tensor_tensor(gn_shift[:, :], gnb_b[:, :], d2, ALU.subtract).then_inc(gn_ok, 1)
            dve.wait_ge(gn_ok, 1)
            end_stage(dve, 3)

            def norm_rows(z, to, rows, tiles, arg, done, count, free, ok):
                for t in range(tiles):
                    ins = dve.bn_stats(bn6[0:rows, t, :], z[:, t, :])
                st.did(ins)
                st.wait()
                alone(dve)
                for t in range(tiles):
                    ins = dve.bn_aggr(bn2[0:rows, t, :], bn6[0:rows, t, :])
                st.did(ins)
                st.wait()
                dve.tensor_scalar(rstd[0:rows, 0, 0:tiles], bn2[0:rows, 0:tiles, 1], EPS, None, ALU.add).then_inc(arg, 1)
                dve.wait_ge(done, count)
                st.did(dve.reciprocal(rstd[0:rows, 0, 0:tiles], rstd[0:rows, 1, 0:tiles]))
                st.wait()
                after(dve, *free)
                for t in range(tiles):
                    ins = dve.tensor_scalar(to[:, t, :], z[:, t, :], bn2[0:rows, t, 0:1], rstd[0:rows, 0, t:t + 1],
                                            ALU.subtract, ALU.mult)
                ins.then_inc(ok, 1)

            def norm_first(i, s, rows, tiles):
                dve.wait_ge(nx_in[s], 32 * (i + 1))
                a, xs, y, z = (tiles_of(k)[0:rows, 0:tiles, :] for k in (s, 2 + s, 6, 9))
                st.did(dve.tensor_tensor(y, a, over_tiles(gn_scale[0:rows, :], rows, tiles), ALU.mult))
                st.wait()
                dve.tensor_tensor(y, y, over_tiles(gn_shift[0:rows, :], rows, tiles), ALU.add).then_inc(nx_y, 1)
                dve.wait_ge(nx_y, 2 * i + s + 1)
                dve.scalar_tensor_tensor(z, y, 0.0, xs, ALU.max, ALU.add).then_inc(nx_used[s], 1)
                dve.wait_ge(nx_used[s], i + 1)
                dve.wait_ge(nx_e, 2 * i + s + 1)
                st.did(dve.scalar_tensor_tensor(z, tiles_of(7)[0:rows, 0:tiles, :], -1.0, z, ALU.add, ALU.add))
                st.wait()
                norm_rows(z, tiles_of(4 + s)[0:rows, 0:tiles, :], rows, tiles, nx_v, nx_r, 2 * i + s + 1,
                          (nx_out[s], 16 * i), nx_ok[s])
            node_groups(dve, norm_first, st)
            end_stage(dve, 4)

            for l in range(LAYERS):
                r = rel[l]
                rows_h = lambda s: tiles_of(4 + s)[:, 0:EG, :]
                st.did(dve.memset(rows_h(1)[:, EG - 1, :], 0.0))
                st.wait()

                def messages(i, s):
                    at = bass.ds((2 * i + s) * EG, EG)
                    st.did(dve.tensor_copy(coef_st[:, s, :, 0:BASES], coef[:, l, at, :]))
                    st.did(dve.tensor_copy(coef_st[:, s, :, BASES], cont[:, at]))
                    st.wait()
                    after(dve, r["out"][s], 16 * EG * i)
                    after(dve, r["row"][1 - s], i + s)
                    for t in range(EG):
                        k = s * EG + t
                        y = psum[2 + k % 2]
                        o = rows_h(s)[:, t, :]
                        prev = rows_h(s)[:, t - 1, :] if t else rows_h(1 - s)[:, EG - 1, :]
                        use = EG * i + k // 2 + 1
                        after(dve, r["y_ps"][k % 2], use)
                        st.did(dve.tensor_scalar(o, y[:, 0:D], coef_st[:, s, t, 0:1], None, ALU.mult))
                        st.wait()
                        for b in range(1, BASES):
                            ins = dve.scalar_tensor_tensor(o, y[:, b * D:(b + 1) * D], coef_st[:, s, t, b:b + 1], o,
                                                           ALU.mult, ALU.add)
                            if b < BASES - 1:
                                st.did(ins)
                                st.wait()
                        ins.then_inc(r["y_used"][k % 2], 1)
                        after(dve, r["y_used"][k % 2], use)
                        ins = dve.scalar_tensor_tensor(o, prev, coef_st[:, s, t, BASES:BASES + 1], o, ALU.mult, ALU.add)
                        if t < EG - 1:
                            st.did(ins)
                            st.wait()
                    ins.then_inc(r["row"][s], 1)
                def message_pair(i):
                    messages(i, 0)
                    messages(i, 1)
                in_pairs(dve, message_pair, EITER, st)
                dve.wait_ge(r["fix_in"], 16)
                dve.wait_ge(r["fix_mm"], 1)
                dve.tensor_tensor(fix[:, 1, 0:D], fix[:, 0, 0:D], psum[0][:, 0:D], ALU.add).then_inc(r["fix_row"], 1)
                end_stage(dve, 5 + 2 * l)

                def update(i, s, rows, tiles):
                    dve.wait_ge(r["n_in"][s], (32 + 16 * l) * (i + 1))
                    after(dve, r["nh_ok" if l == 0 else "h_ok"][s], i)
                    for c, t0, n in chunks(tiles):
                        b = c % 2
                        dve.wait_ge(r["nm_ps"][b], 4 * i + 2 * s + c // 2 + 1)
                        dve.tensor_tensor(work[10 + s][0:rows, t0 * D:(t0 + n) * D], psum[2 + b][0:rows, 0:n * D],
                                          work[s][0:rows, t0 * D:(t0 + n) * D], ALU.add).then_inc(r["nm_used"][b], 1)
                    wait_group(dve, r["nm_used"], i, s, tiles)
                    total = tiles_of(10 + s)[0:rows, 0:tiles, :]
                    dve.tensor_tensor(total, total, over_tiles(bias_b[0:rows, l, :], rows, tiles), ALU.add).then_inc(r["s_ok"][s], 1)
                    if l == LAYERS - 1:
                        z = tiles_of(12 + s)[0:rows, 0:tiles, :]
                        dve.wait_ge(r["h_ok"][s], i + 1)
                        dve.tensor_tensor(z, z, tiles_of(4 + s)[0:rows, 0:tiles, :], ALU.add).then_inc(r["z_ok"][s], 1)
                        dve.wait_ge(r["z_ok"][s], i + 1)
                        norm_rows(z, tiles_of(6 + s)[0:rows, 0:tiles, :], rows, tiles, r["v_ok"], r["r_ok"], 2 * i + s + 1,
                                  (r["nh_out"][s], 16 * i), r["nh_ok"][s])
                node_groups(dve, update, st)
                end_stage(dve, 6 + 2 * l)


_INS = ['x', 'src', 'dst', 'edge_type_32', 'L0_gnn_Wl', 'L0_gnn_Wr', 'L0_gnn_att', 'L0_gnn_bias_conv',
        'L0_gnn_gn_weight', 'L0_gnn_gn_bias', 'L0_gnn_gn_mean_scale', 'L1_gnn_basis', 'L1_gnn_comp',
        'L1_gnn_loop_w', 'L1_gnn_bias']


def kernel(**inputs):
    import numpy as _np
    import concourse.bacc as _bacc
    from concourse import mybir as _mybir
    from concourse.bass_utils import run_bass_kernel_spmd as _run

    nc = _bacc.Bacc("TRN2", target_bir_lowering=False, num_devices=1)
    arrays, args = {}, []
    for name in _INS:
        a = _np.ascontiguousarray(inputs[name])
        arrays[f"in_{name}_dram"] = a
        args.append(nc.dram_tensor(f"in_{name}_dram", a.shape, _mybir.dt.from_np(a.dtype), kind="ExternalInput").ap())
    args.append(nc.dram_tensor("out_0_dram", (N, D), _mybir.dt.float32, kind="ExternalOutput").ap())
    gnn_kernel(nc, *args)
    r = _run(nc, [arrays], core_ids=[0])
    return r.results[0]["out_0_dram"]
```

```python
from contextlib import ExitStack

import concourse.bass as bass
from concourse import mybir

F32 = mybir.dt.float32
I32 = mybir.dt.int32
ALU = mybir.AluOpType
ACT = mybir.ActivationFunctionType
AX = mybir.AxisListType

P = 128
D = 128
H = 4
C = D // H
BASES = 4
RELS = 32
LAYERS = 2
N = 50000
E = 50000

NT = 13
GROUP = NT * P
NG = N // GROUP
TAIL = N - NG * GROUP
LAST = NG // 2
NODE_TILES = NG * NT + 1

ET = 392
EG = 7
EGROUPS = ET // EG
EITER = EGROUPS // 2
FULL_E = (P - 1) * ET
REST_E = E - FULL_E

EPAD = P * ET
CT = -(-ET // LAST)
NODE_ROUND = 16 * NT

ROW = D + 2 * H
FAR = 65536
PAD_DST = 65535
LOW = 1e30
SLOPE = 0.2
EPS = 1e-5


def chunks(tiles):
    return [(c, t, min(4, tiles - t)) for c, t in enumerate(range(0, tiles, 4))]


def after(eng, sem, count):
    if not isinstance(count, int) or count > 0:
        eng.wait_ge(sem, count)


def wait_group(eng, bank_sems, i, s, tiles):
    eng.wait_ge(bank_sems[0], 4 * i + 2 * s + (2 if tiles > 8 else 1))
    if tiles > 4:
        eng.wait_ge(bank_sems[1], 4 * i + 2 * s + (2 if tiles > 12 else 1))


YBANKS = 5
EDGE_CHUNKS = [(0, 0, 4), (1, 4, EG - 4)]


class Steps:

    def __init__(self, eng, sem):
        self.eng, self.sem, self.base, self.n, self.turns, self.per = eng, sem, 0, 0, None, 0

    def enter(self, turns, per):
        self.base, self.n, self.turns, self.per = self.base + self.n, 0, turns, per

    def leave(self, rounds):
        assert self.n == self.per, (self.n, self.per)
        self.base, self.n, self.turns = self.base + self.per * rounds, 0, None

    def did(self, ins):
        ins.then_inc(self.sem, 1)
        self.n += 1

    def wait(self, upto=None):
        at = self.base + (self.n if upto is None else upto)
        self.eng.wait_ge(self.sem, at if self.turns is None else self.turns * self.per + at)


def in_pairs(eng, pair, rounds, steps=None):
    before = steps.n if steps else 0
    pair(0)
    per = steps.n - before if steps else 0
    with eng.Fori(1, rounds) as i:
        if steps:
            steps.enter(i - 1, per)
        pair(i)
    if steps:
        steps.leave(rounds - 1)


def node_groups(eng, body, steps=None):
    def pair(i):
        body(i, 0, P, NT)
        body(i, 1, P, NT)
    in_pairs(eng, pair, LAST, steps)
    body(LAST, 0, TAIL, 1)


def node_steps(eng, first, step, steps=None):
    def pair(i):
        step((i, 0, P, NT), (i, 1, P, NT))
        step((i, 1, P, NT), (i + 1, 0, P, NT))
    first(0, 0, P, NT)
    in_pairs(eng, pair, LAST - 1, steps)
    step((LAST - 1, 0, P, NT), (LAST - 1, 1, P, NT))
    step((LAST - 1, 1, P, NT), (LAST, 0, TAIL, 1))
    step((LAST, 0, TAIL, 1), None)


def node_rows(dram, i, s, rows, tiles):
    if rows == P:
        part = dram[bass.ds((2 * i + s) * GROUP, GROUP), :]
    else:
        part = dram[NG * GROUP:N, :]
    return part.rearrange("(p t) d -> p (t d)", t=tiles)


def gnn_kernel(nc, x, src, dst, etype, Wl, Wr, att, bias_conv, gn_weight, gn_bias, gn_mean_scale,
               basis, comp, loop_w, bias, out):
    ctx = ExitStack()
    with ctx:
        def sb(name, shape, dt=F32):
            return ctx.enter_context(nc.sbuf_tensor(name, shape, dt))

        def sem(name):
            return ctx.enter_context(nc.semaphore(name))

        def sems(name):
            return [sem(f"{name}{k}") for k in range(2)]

        xl_d = nc.dram_tensor("xl_d", [N, D], F32).ap()
        xr_d = nc.dram_tensor("xr_d", [N, D], F32).ap()
        gat_d = nc.dram_tensor("gat_d", [EPAD + P, ROW], F32).ap()
        conv_d = nc.dram_tensor("conv_d", [N, D], F32).ap()
        x1_d = nc.dram_tensor("x1_d", [N, D], F32).ap()
        agg_d = nc.dram_tensor("agg_d", [EPAD + P, D], F32).ap()
        last_d = nc.dram_tensor("last_d", [N, 1], I32).ap()
        h1_d = nc.dram_tensor("h1_d", [N, D], F32).ap()

        src_i = sb("src_i", [P, ET], I32)
        dst_i = sb("dst_i", [P, ET], I32)
        next_i = sb("next_i", [P, ET], I32)
        etype_i = sb("etype_i", [P, CT * LAST], I32)
        edge_id = sb("edge_id", [P, ET], I32)
        no_edge = sb("no_edge", [P, NG * NT], I32)
        node_idx = sb("node_idx", [P, NODE_TILES], I32)
        xr_idx = sb("xr_idx", [P, ET], I32)
        out_idx = sb("out_idx", [P, ET], I32)
        cont = sb("cont", [P, ET])
        drop = sb("drop", [P, ET])
        coef = sb("coef", [P, LAYERS, CT * LAST, BASES])
        self_logit = sb("self_logit", [P, NODE_TILES, H])
        ident = sb("ident", [P, P])
        ones = sb("ones", [P, P])
        w_lr = sb("w_lr", [D, 2 * D])
        att_b = sb("att_b", [P, D])
        conv_b = sb("conv_b", [P, D])
        gnw_b = sb("gnw_b", [P, D])
        gnb_b = sb("gnb_b", [P, D])
        gms_b = sb("gms_b", [P, D])
        bias_b = sb("bias_b", [P, LAYERS, D])
        comp_b = sb("comp_b", [P, LAYERS, RELS, BASES])
        basis_s = sb("basis_s", [D, LAYERS, BASES, D])
        loop_s = sb("loop_s", [D, LAYERS, D])
        rel_id = sb("rel_id", [P, RELS])
        gn_scale = sb("gn_scale", [P, D])
        gn_shift = sb("gn_shift", [P, D])
        stat = sb("stat", [P, 6, D])
        next_last = sb("next_last", [P, 1], I32)
        after_next = sb("after_next", [P, 1], I32)
        last_f = sb("last_f", [P, 1])
        flag = sb("flag", [P, 4])
        fix_node = sb("fix_node", [P, 1], I32)
        fix_idx = sb("fix_idx", [P, 1], I32)
        edge_m = sb("edge_m", [P, 3, P])
        fix = sb("fix", [P, 2, ROW])
        fix_s = sb("fix_s", [P, 8, H])
        diag = sb("diag", [P, H, P])
        idx_st = sb("idx_st", [P, 2, 2, EG], I32)
        node_st = sb("node_st", [P, 2, NT], I32)
        drop_st = sb("drop_st", [P, 2, EG])
        coef_st = sb("coef_st", [P, 2, EG, BASES + 1])
        logit = sb("logit", [P, EG, H])
        exp_in = sb("exp_in", [P, 2, EG, H])
        exp_out = sb("exp_out", [P, 2, EG, H])
        nexp_in = sb("nexp_in", [P, 2, NT, H])
        nexp_out = sb("nexp_out", [P, 2, NT, H])
        nsm = sb("nsm", [P, 3, NT, H])
        bn6 = sb("bn6", [P, NT, 6])
        bn2 = sb("bn2", [P, NT, 2])
        rstd = sb("rstd", [P, 2, NT])
        work = [sb(f"work{k}", [P, NT * ROW]) for k in range(14)]

        lr = sb("lr", [P, 2, NT, 2 * D])

        def tiles_of(k, tiles=NT, width=D):
            return work[k][:, 0:tiles * width].rearrange("p (t d) -> p t d", d=width)

        psum = [ctx.enter_context(nc.psum_tensor(f"bank{k}", [P, 512], F32)) for k in range(8)]

        cleared = sem("cleared")
        tables_in = sem("tables_in")
        weights_in = sem("weights_in")
        consts = sem("consts")
        tables_ok = sem("tables_ok")
        filled = sem("filled")
        default_ok = sem("default_ok")
        last_out = sems("last_out")
        node_idx_in = sem("node_idx_in")
        fix_idx_in = sem("fix_idx_in")
        stage_done = sem("stage_done")
        passed = sem("passed")
        dve_steps = sem("dve_steps")
        pool_steps = sem("pool_steps")
        act_steps = sem("act_steps")

        x_in, x_used = sems("x_in"), sems("x_used")
        xt_ps, xt_cp = sems("xt_ps"), sems("xt_cp")
        lr_ps, l_cp, r_cp, l_read, lr_out = sems("lr_ps"), sems("l_cp"), sems("r_cp"), sems("l_read"), sems("lr_out")
        at_in, at_row, at_out = sems("at_in"), sems("at_row"), sems("at_out")
        at_arg, at_exp = sem("at_arg"), sem("at_exp")
        fix_rd, fix_mm, fix_act, fix_in, fix_out, fixed = (
            sem("fix_rd"), sem("fix_mm"), sem("fix_act"), sem("fix_in"), sem("fix_out"), sem("fixed"))
        ag_in, ag_used, cv_ok, cv_sq, cv_mm, cv_out = (
            sems("ag_in"), sems("ag_used"), sems("cv_ok"), sems("cv_sq"), sems("cv_mm"), sems("cv_out"))
        ag_arg, ag_exp, ag_row = sem("ag_arg"), sem("ag_exp"), sems("ag_row")
        zeroed, gn_var, gn_std, gn_ok = sem("zeroed"), sem("gn_var"), sem("gn_std"), sem("gn_ok")
        nx_in, nx_used, nx_ok, nx_out = sems("nx_in"), sems("nx_used"), sems("nx_ok"), sems("nx_out")
        nx_y, nx_e, nx_v, nx_r = sem("nx_y"), sem("nx_e"), sem("nx_v"), sem("nx_r")
        rel = []
        for l in range(LAYERS):
            rel.append({n: sems(f"r{l}_{n}") for n in (
                "h_in", "t_ps", "t_cp", "row", "out",
                "n_in", "n_row", "nt_ps", "nt_cp", "nm_ps", "nm_used", "s_ok", "nh_ok", "nh_out",
                ) + (("h_ok", "z_ok") if l else ())} | {n: sem(f"r{l}_{n}") for n in ("y_ps", "y_used") + (("v_ok", "r_ok") if l else ())})

        def alone(eng):
            eng.sem_inc(passed, 1)

        def end_stage(eng, k):
            eng.drain().then_inc(stage_done, 1)
            eng.wait_ge(stage_done, 5 * k)

        block = ctx.enter_context(nc.Block())

        edge_rows = lambda a, o=0: a[o:o + FULL_E].rearrange("(p t) -> p t", t=ET)

        @block.sync
        def _(sp):
            sp.dma_start(w_lr[:, 0:D], Wl).then_inc(weights_in, 16)
            sp.dma_start(w_lr[:, D:2 * D], Wr).then_inc(weights_in, 16)
            for tile, row in ((att_b[:, :], att.rearrange("h c -> (h c)")), (conv_b[:, :], bias_conv),
                              (gnw_b[:, :], gn_weight), (gnb_b[:, :], gn_bias), (gms_b[:, :], gn_mean_scale),
                              (bias_b[:, :, :].rearrange("p l d -> p (l d)"), bias.rearrange("l d -> (l d)")),
                              (comp_b[:, :, :, :].rearrange("p l r b -> p (l r b)"),
                               comp.rearrange("l r b -> (l r b)"))):
                sp.dma_start(tile, row.partition_broadcast(P)).then_inc(weights_in, 16)
            sp.dma_start(basis_s[:, :, :, :], basis.rearrange("l b k n -> k l b n")).then_inc(weights_in, 16)
            sp.dma_start(loop_s[:, :, :], loop_w.rearrange("l k n -> k l n")).then_inc(weights_in, 16)
            sp.wait_ge(cleared, 6)
            for tile, a, o in ((src_i, src, 0), (dst_i, dst, 0), (etype_i, etype, 0), (next_i, dst, 1)):
                sp.dma_start(tile[0:P - 1, 0:ET], edge_rows(a, o)).then_inc(tables_in, 16)
                sp.dma_start(tile[P - 1:P, 0:REST_E - o],
                             a[FULL_E + o:E].rearrange("(p t) -> p t", p=1)).then_inc(tables_in, 16)
            sp.dma_start(next_last[0:P - 2, :], edge_rows(dst)[1:P - 1, ET - 1:ET],
                         allow_slow_non_contiguous=True).then_inc(tables_in, 16)
            sp.dma_start(after_next[0:P - 2, :], dst[ET + 1:ET + 1 + (P - 2) * ET]
                         .rearrange("(p t) -> p t", t=ET)[:, ET - 1:ET],
                         allow_slow_non_contiguous=True).then_inc(tables_in, 16)

            sp.wait_ge(default_ok, 2)
            sp.dma_start(gat_d[EPAD:EPAD + P, :], work[12][:, 0:ROW]).then_inc(filled, 16)
            sp.dma_start(agg_d[EPAD:EPAD + P, :], work[13][:, 0:D]).then_inc(filled, 16)
            sp.wait_ge(consts, 5)
            sp.dma_start(last_d[0:NG * GROUP, :].rearrange("(p t) o -> p (t o)", p=P), no_edge[:, :]).then_inc(filled, 16)
            sp.dma_start(last_d[NG * GROUP:N, :], no_edge[0:TAIL, 0:1]).then_inc(filled, 16)

            def stream(load, store):
                def pair(i):
                    for s in range(2):
                        load(i + 1, s, P, NT)
                        store(i, s, P, NT)
                for s in range(2):
                    load(0, s, P, NT)
                in_pairs(sp, pair, LAST - 1)
                load(LAST, 0, TAIL, 1)
                for s in range(2):
                    store(LAST - 1, s, P, NT)
                store(LAST, 0, TAIL, 1)

            def load(dram, k, into, i, s, rows, tiles):
                sp.dma_start(work[k + s][0:rows, 0:tiles * D], node_rows(dram, i, s, rows, tiles)).then_inc(into[s], 16)

            def save(dram, k, done, i, s, rows, tiles):
                sp.dma_start(node_rows(dram, i, s, rows, tiles), work[k + s][0:rows, 0:tiles * D]).then_inc(done[s], 16)

            def stored(done, each=16):
                sp.wait_ge(done[0], each * (LAST + 1))
                sp.wait_ge(done[1], each * LAST)

            def load_x(i, s, rows, tiles):
                after(sp, x_used[s], i)
                load(x, 0, x_in, i, s, rows, tiles)

            def save_lr(i, s, rows, tiles):
                wait_group(sp, r_cp, i, s, tiles)
                wait_group(sp, l_cp, i, s, tiles)
                for k, dram in enumerate((xl_d, xr_d)):
                    sp.dma_start(node_rows(dram, i, s, rows, tiles).rearrange("p (t d) -> p t d", d=D),
                                 lr[0:rows, s, 0:tiles, k * D:(k + 1) * D]).then_inc(lr_out[s], 16)
            stream(load_x, save_lr)
            stored(lr_out, 32)
            end_stage(sp, 1)

            sp.dma_start(node_idx[:, 0:NG * NT].rearrange("p (g t) -> p g t", t=NT),
                         last_d[0:NG * GROUP, :].rearrange("(g p t) o -> p g (t o)", p=P, t=NT)).then_inc(node_idx_in, 16)
            sp.dma_start(node_idx[0:TAIL, NG * NT:NODE_TILES], last_d[NG * GROUP:N, :]).then_inc(node_idx_in, 16)
            sp.wait_ge(node_idx_in, 32)

            def save_rows(dram, k, width, ready, done):
                by_edge = dram[0:EPAD, :].rearrange("(p t) d -> p t d", t=ET)

                def pair(i):
                    for s in range(2):
                        sp.wait_ge(ready[s], i + 1)
                        sp.dma_start(by_edge[:, bass.ds((2 * i + s) * EG, EG), :].rearrange("p t d -> p (t d)"),
                                     work[k + s][:, 0:EG * width]).then_inc(done[s], 16)
                in_pairs(sp, pair, EITER)
                for s in range(2):
                    sp.wait_ge(done[s], 16 * EITER)
            save_rows(gat_d, 4, ROW, at_row, at_out)
            sp.wait_ge(fix_out, 16)
            end_stage(sp, 2)

            def load_xl(i, s, rows, tiles):
                after(sp, ag_used[s], i)
                load(xl_d, 2, ag_in, i, s, rows, tiles)

            def save_cv(i, s, rows, tiles):
                sp.wait_ge(cv_ok[s], i + 1)
                save(conv_d, 4, cv_out, i, s, rows, tiles)
            stream(load_xl, save_cv)
            stored(cv_out)
            end_stage(sp, 3)

            def load_nx(i, s, rows, tiles):
                after(sp, nx_used[s], i)
                load(conv_d, 0, nx_in, i, s, rows, tiles)
                load(x, 2, nx_in, i, s, rows, tiles)

            def save_nx(i, s, rows, tiles):
                sp.wait_ge(nx_ok[s], i + 1)
                save(x1_d, 4, nx_out, i, s, rows, tiles)
            stream(load_nx, save_nx)
            stored(nx_out)
            end_stage(sp, 4)

            for l in range(LAYERS):
                r = rel[l]
                save_rows(agg_d, 4, D, r["row"], r["out"])
                sp.wait_ge(fix_out, 16 * (2 + l))
                end_stage(sp, 5 + 2 * l)

                def load_n(i, s, rows, tiles):
                    after(sp, r["s_ok" if l == 0 else "z_ok"][s], i)
                    load((x1_d, h1_d)[l], 2, r["n_in"], i, s, rows, tiles)
                    if l == LAYERS - 1:
                        load(x1_d, 4, r["n_in"], i, s, rows, tiles)

                def save_n(i, s, rows, tiles):
                    sp.wait_ge(r["nh_ok"][s], i + 1)
                    save((h1_d, out)[l], 6, r["nh_out"], i, s, rows, tiles)
                stream(load_n, save_n)
                stored(r["nh_out"])
                end_stage(sp, 6 + 2 * l)

        @block.gpsimd
        def _(pool):
            st = Steps(pool, pool_steps)
            pool.iota(rel_id[:, :], [[1, RELS]], base=0, channel_multiplier=0,
                      allow_small_or_imprecise_dtypes=True).then_inc(consts, 1)
            st.did(pool.memset(ident[:, :], 0.0))
            st.wait()
            pool.affine_select(out=ident[:, :], in_=ident[:, :], compare_op=ALU.not_equal, fill=1.0,
                               base=0, pattern=[[-1, P]], channel_multiplier=1).then_inc(consts, 1)
            pool.memset(ones[:, :], 1.0).then_inc(consts, 1)

            st.did(pool.iota(edge_id[:, :], [[1, ET]], base=0, channel_multiplier=ET))
            pool.iota(no_edge[:, :], [[0, NG * NT]], base=EPAD, channel_multiplier=1).then_inc(consts, 1)
            pool.sem_inc(consts, 1)

            def stage_idx(k, table, i, s):
                st.did(pool.tensor_copy(idx_st[:, s, k, :], table[:, bass.ds((2 * i + s) * EG, EG)]))

            def column(s, k, t):
                return bass.IndirectOffsetOnAxis(ap=idx_st[:, s, k, t:t + 1], axis=0)

            pool.wait_ge(tables_ok, 1)
            pool.wait_ge(filled, 16 * 4)

            def last_edges(i):
                for s in range(2):
                    after(pool, last_out[s], 16 * EG * i)
                    stage_idx(0, out_idx, i, s)
                    stage_idx(1, edge_id, i, s)
                    st.wait()
                    alone(pool)
                    for t in range(EG):
                        pool.indirect_dma_start(last_d, column(s, 0, t), idx_st[:, s, 1, t:t + 1], None,
                                                bounds_check=N - 1, oob_is_err=False).then_inc(last_out[s], 16)
            in_pairs(pool, last_edges, EITER, st)
            for s in range(2):
                pool.wait_ge(last_out[s], 16 * EG * EITER)
            pool.indirect_dma_start(fix_idx[:, :], None, last_d, bass.IndirectOffsetOnAxis(ap=fix_node[:, 0:1], axis=0),
                                    bounds_check=N - 1, oob_is_err=False).then_inc(fix_idx_in, 16)
            pool.wait_ge(fix_idx_in, 16)
            end_stage(pool, 1)

            def gather_at(i):
                for s in range(2):
                    after(pool, at_row[s], i)
                    stage_idx(0, src_i, i, s)
                    stage_idx(1, xr_idx, i, s)
                    st.wait()
                    alone(pool)
                    for t in range(EG):
                        for k, dram in enumerate((xl_d, xr_d)):
                            pool.indirect_dma_start(tiles_of(2 * k + s)[:, t, :], None, dram, column(s, k, t)).then_inc(at_in[s], 16)
            in_pairs(pool, gather_at, EITER, st)
            by_fix = bass.IndirectOffsetOnAxis(ap=fix_idx[:, 0:1], axis=0)
            for s in range(2):
                pool.wait_ge(at_out[s], 16 * EITER)
            pool.wait_ge(fixed, 1)
            pool.indirect_dma_start(fix[:, 0, :], None, gat_d, by_fix, bounds_check=EPAD - 1, oob_is_err=False).then_inc(fix_in, 16)
            pool.wait_ge(fixed, 2)
            pool.indirect_dma_start(gat_d, by_fix, fix[:, 1, :], None, bounds_check=EPAD - 1, oob_is_err=False).then_inc(fix_out, 16)
            pool.wait_ge(fix_out, 16)
            end_stage(pool, 2)

            def gather_nodes(dram, width, free, into):
                def group(i, s, rows, tiles):
                    after(pool, free[s], i)
                    at = bass.ds((2 * i + s) * NT, NT) if rows == P else slice(NG * NT, NODE_TILES)
                    st.did(pool.tensor_copy(node_st[0:rows, s, 0:tiles], node_idx[0:rows, at]))
                    st.wait()
                    alone(pool)
                    for t in range(tiles):
                        pool.indirect_dma_start(tiles_of(s, NT, width)[0:rows, t, :], None, dram,
                                                bass.IndirectOffsetOnAxis(ap=node_st[0:rows, s, t:t + 1], axis=0)).then_inc(into[s], 16)
                node_groups(pool, group, st)
            gather_nodes(gat_d, ROW, ag_used, ag_row)
            end_stage(pool, 3)
            end_stage(pool, 4)

            for l in range(LAYERS):
                r = rel[l]

                def gather_h(i):
                    for s in range(2):
                        after(pool, r["t_ps"][1], 2 * i + s - 1)
                        stage_idx(0, src_i, i, s)
                        st.wait()
                        alone(pool)
                        for t in range(EG):
                            pool.indirect_dma_start(tiles_of(s)[:, t, :], None, (x1_d, h1_d)[l], column(s, 0, t)).then_inc(r["h_in"][s], 16)
                in_pairs(pool, gather_h, EITER, st)
                for s in range(2):
                    pool.wait_ge(r["out"][s], 16 * EITER)
                pool.indirect_dma_start(fix[:, 0, 0:D], None, agg_d, by_fix, bounds_check=EPAD - 1, oob_is_err=False).then_inc(fix_in, 16)
                pool.wait_ge(fixed, 3 + l)
                pool.indirect_dma_start(agg_d, by_fix, fix[:, 1, 0:D], None, bounds_check=EPAD - 1, oob_is_err=False).then_inc(fix_out, 16)
                pool.wait_ge(fix_out, 16 * (2 + l))
                end_stage(pool, 5 + 2 * l)
                gather_nodes(agg_d, D, r["s_ok"], r["n_row"])
                end_stage(pool, 6 + 2 * l)

        @block.tensor
        def _(pe):
            pe.wait_ge(consts, 3)
            pe.wait_ge(weights_in, 16 * 11)

            def transpose_chunk(tiles, rows, c, t0, n, use, ps, cp):
                after(pe, cp[c % 2], use)
                for t in range(t0, t0 + n):
                    last = pe.transpose(psum[c % 2][:, (t - t0) * P:(t - t0) * P + rows],
                                        tiles[0:rows, t, :], ident[0:rows, 0:rows])
                last.then_inc(ps[c % 2], 1)

            def project(i, s, rows, tiles):
                pe.wait_ge(x_in[s], 16 * (i + 1))
                todo = chunks(tiles)

                def multiply(c, t0, n):
                    use = 4 * i + 2 * s + c // 2
                    b = c % 2
                    pe.wait_ge(xt_cp[b], use + 1)
                    after(pe, l_cp[b], use)
                    after(pe, r_cp[b], use)
                    for t in range(t0, t0 + n):
                        k = t - t0
                        last = pe.matmul(psum[2 + 2 * b + k // 2][0:rows, (k % 2) * 256:(k % 2) * 256 + 256],
                                         tiles_of(8 + s)[:, t, 0:rows], w_lr[:, :], start=True, stop=True)
                        if c == len(todo) - 2 and k == 0:
                            last.then_inc(x_used[s], 1)
                    last.then_inc(lr_ps[b], 1)

                for c, t0, n in todo:
                    transpose_chunk(tiles_of(s), rows, c, t0, n, 4 * i + 2 * s + c // 2, xt_ps, xt_cp)
                    if c:
                        multiply(*todo[c - 1])
                multiply(*todo[-1])
            node_groups(pe, project)
            end_stage(pe, 1)

            pe.wait_ge(fix_rd, 1)
            pe.matmul(psum[0][:, 0:P], ones[:, :], edge_m[:, 0, :], start=True, stop=True)
            pe.matmul(psum[0][:, P:2 * P], ones[:, :], edge_m[:, 1, :], start=True, stop=True)
            pe.matmul(psum[1][:, :], ones[:, :], diag[:, :, :].rearrange("p h q -> p (h q)"), start=True, stop=True).then_inc(fix_mm, 1)
            pe.wait_ge(fix_rd, 3)
            pe.matmul(psum[2][:, 0:D + H], edge_m[:, 0, :], work[10][:, 0:D + H], start=True, stop=True).then_inc(fix_mm, 1)
            end_stage(pe, 2)

            pe.wait_ge(zeroed, 1)
            for b in range(2):
                pe.matmul(psum[b][:, :], ones[:, :], work[12][:, 0:512], start=True, stop=False, skip_group_check=True)

            def sums(i, s, rows, tiles):
                for b, (sig, k) in enumerate(((cv_ok, 4), (cv_sq, 6))):
                    pe.wait_ge(sig[s], i + 1)
                    for c, t0, n in chunks(tiles):
                        last = pe.matmul(psum[b][:, 0:n * D], ones[0:rows, :],
                                         work[k + s][0:rows, t0 * D:(t0 + n) * D], start=False, stop=False,
                                         skip_group_check=True)
                last.then_inc(cv_mm[s], 1)
            node_groups(pe, sums)
            end_stage(pe, 3)
            end_stage(pe, 4)

            for l in range(LAYERS):
                r = rel[l]

                def turn(i, s):
                    pe.wait_ge(r["h_in"][s], 16 * EG * (i + 1))
                    for c, t0, n in EDGE_CHUNKS:
                        after(pe, r["t_cp"][c], 2 * i + s)
                        for t in range(t0, t0 + n):
                            last = pe.transpose(psum[c][:, (t - t0) * P:(t - t0 + 1) * P], tiles_of(s)[:, t, :], ident[:, :])
                        last.then_inc(r["t_ps"][c], 1)

                def expand(i, s):
                    for c, t0, n in EDGE_CHUNKS:
                        pe.wait_ge(r["t_cp"][c], 2 * i + s + 1)
                        for t in range(t0, t0 + n):
                            k = s * EG + t
                            user = 2 * EG * i + k - YBANKS if k >= YBANKS else (
                                2 * EG * (i - 1) + max(q for q in range(2 * EG) if q % YBANKS == k))
                            after(pe, r["y_used"], user + 1)
                            pe.matmul(psum[2 + k % YBANKS][:, :], tiles_of(2 + s)[:, t, :],
                                      basis_s[:, l, :, :].rearrange("k b n -> k (b n)"), start=True, stop=True).then_inc(r["y_ps"], 1)

                def edge_pair(i):
                    turn(i, 1)
                    expand(i, 0)
                    turn(i + 1, 0)
                    expand(i, 1)
                turn(0, 0)
                in_pairs(pe, edge_pair, EITER - 1)
                turn(EITER - 1, 1)
                expand(EITER - 1, 0)
                expand(EITER - 1, 1)
                pe.wait_ge(r["row"][1], EITER)
                pe.matmul(psum[0][:, 0:D], edge_m[:, 0, :], tiles_of(5)[:, EG - 1, :], start=True, stop=True).then_inc(fix_mm, 1)
                end_stage(pe, 5 + 2 * l)

                def nodes(i, s, rows, tiles):
                    pe.wait_ge(r["n_in"][s], (16 + 16 * l) * (i + 1))
                    todo = chunks(tiles)

                    def multiply(c, t0, n):
                        use, b = 4 * i + 2 * s + c // 2, c % 2
                        pe.wait_ge(r["nt_cp"][b], use + 1)
                        after(pe, r["nm_used"][b], use)
                        pe.matmul(psum[2 + b][0:rows, 0:n * D], ones[0:1, 0:rows],
                                  bias_b[0:1, l, :].unsqueeze(1).to_broadcast([1, n, D]), start=True, stop=False)
                        for t in range(t0, t0 + n):
                            last = pe.matmul(psum[2 + b][0:rows, (t - t0) * D:(t - t0 + 1) * D],
                                             tiles_of(8 + s)[:, t, 0:rows], loop_s[:, l, :],
                                             start=False, stop=(t == t0 + n - 1))
                        last.then_inc(r["nm_ps"][b], 1)

                    for c, t0, n in todo:
                        transpose_chunk(tiles_of(2 + s), rows, c, t0, n, 4 * i + 2 * s + c // 2, r["nt_ps"], r["nt_cp"])
                        if c:
                            multiply(*todo[c - 1])
                    multiply(*todo[-1])
                node_groups(pe, nodes)
                end_stage(pe, 6 + 2 * l)

        @block.scalar
        def _(act):
            st = Steps(act, act_steps)

            def copy_turned(i, s, rows, n, c, t0, k, ps, cp):
                act.wait_ge(ps[c % 2], 4 * i + 2 * s + c // 2 + 1)
                act.activation(tiles_of(k + s)[:, t0:t0 + n, 0:rows],
                               psum[c % 2][:, 0:n * P].rearrange("p (t d) -> p t d", d=P)[:, :, 0:rows],
                               ACT.Copy).then_inc(cp[c % 2], 1)

            def project(i, s, rows, tiles):
                todo = chunks(tiles)
                after(act, lr_out[s], 32 * i)
                after(act, l_read[s], i)

                def copy_l(c, t0, n):
                    b, m = c % 2, min(2, n)
                    act.wait_ge(lr_ps[b], 4 * i + 2 * s + c // 2 + 1)
                    act.activation(lr[0:rows, s, t0:t0 + m, :].rearrange("p t d -> p (t d)"),
                                   psum[2 + 2 * b][0:rows, 0:m * 256], ACT.Copy).then_inc(l_cp[b], 1)
                for c, t0, n in todo:
                    copy_turned(i, s, rows, n, c, t0, 8, xt_ps, xt_cp)
                    if c:
                        copy_l(*todo[c - 1])
                copy_l(*todo[-1])
            node_groups(act, project)
            end_stage(act, 1)

            with act.Fori(0, EGROUPS) as g:
                act.wait_ge(at_arg, g + 1)
                act.activation(exp_out[:, :, :, :], exp_in[:, :, :, :], ACT.Exp).then_inc(at_exp, 1)
            act.wait_ge(fix_rd, 2)
            act.activation(fix_s[:, 2, :], fix_s[:, 1, :], ACT.Exp).then_inc(fix_act, 1)
            act.wait_ge(fix_rd, 4)
            act.activation(fix_s[:, 6:8, :], fix_s[:, 4:6, :], ACT.Exp).then_inc(fix_act, 1)
            end_stage(act, 2)

            def exps(i, s, rows, tiles):
                act.wait_ge(ag_arg, 2 * i + s + 1)
                act.activation(nexp_out[0:rows, :, 0:tiles, :], nexp_in[0:rows, :, 0:tiles, :], ACT.Exp).then_inc(ag_exp, 1)

            def squares(group, following):
                i, s, rows, tiles = group
                if following:
                    exps(*following)
                act.wait_ge(cv_ok[s], i + 1)
                after(act, cv_mm[s], i)
                act.activation(work[6 + s][0:rows, 0:tiles * D], work[4 + s][0:rows, 0:tiles * D], ACT.Square).then_inc(cv_sq[s], 1)
            node_steps(act, exps, squares)
            act.wait_ge(gn_var, 1)
            act.activation(stat[:, 5, :], stat[:, 4, :], ACT.Sqrt).then_inc(gn_std, 1)
            end_stage(act, 3)

            def elu_part(i, s, rows, tiles):
                act.wait_ge(nx_y, 2 * i + s + 1)
                w = tiles * D
                st.did(act.activation(work[8][0:rows, 0:w], work[6][0:rows, 0:w], ACT.Relu, scale=-1.0))
                st.wait()
                act.activation(work[7][0:rows, 0:w], work[8][0:rows, 0:w], ACT.Exp, scale=-1.0).then_inc(nx_e, 1)

            def deviation(group, arg, done):
                i, s, rows, tiles = group
                act.wait_ge(arg, 2 * i + s + 1)
                act.activation(rstd[0:rows, 1, 0:tiles], rstd[0:rows, 0, 0:tiles], ACT.Sqrt).then_inc(done, 1)

            def elu_step(group, following):
                deviation(group, nx_v, nx_r)
                if following:
                    elu_part(*following)
            node_steps(act, elu_part, elu_step, st)
            end_stage(act, 4)

            for l in range(LAYERS):
                r = rel[l]

                def turned(i, s):
                    for c, t0, n in EDGE_CHUNKS:
                        act.wait_ge(r["t_ps"][c], 2 * i + s + 1)
                        act.activation(tiles_of(2 + s)[:, t0:t0 + n, :],
                                       psum[c][:, 0:n * P].rearrange("p (t d) -> p t d", d=P),
                                       ACT.Copy).then_inc(r["t_cp"][c], 1)
                def turned_pair(i):
                    turned(i, 0)
                    turned(i, 1)
                in_pairs(act, turned_pair, EITER)
                end_stage(act, 5 + 2 * l)

                def nodes(i, s, rows, tiles):
                    for c, t0, n in chunks(tiles):
                        copy_turned(i, s, rows, n, c, t0, 8, r["nt_ps"], r["nt_cp"])
                    act.wait_ge(r["s_ok"][s], i + 1)
                    if l == 0:
                        after(act, r["nh_out"][s], 16 * i)
                        to, done = work[6 + s], r["nh_ok"]
                    else:
                        after(act, r["nh_ok"][s], i)
                        to, done = work[12 + s], r["h_ok"]
                    act.activation(to[0:rows, 0:tiles * D], work[10 + s][0:rows, 0:tiles * D], ACT.Tanh).then_inc(done[s], 1)

                def node_step(group, following):
                    deviation(group, r["v_ok"], r["r_ok"])
                    if following:
                        nodes(*following)
                if l == 0:
                    node_groups(act, nodes)
                else:
                    node_steps(act, nodes, node_step)
                end_stage(act, 6 + 2 * l)

        @block.vector
        def _(dve):
            st = Steps(dve, dve_steps)

            def over_tiles(row, rows, tiles):
                return row.unsqueeze(1).to_broadcast([rows, tiles, D])

            def per_head(small):
                a = small.unsqueeze(len(small.shape))
                return a.to_broadcast(list(small.shape) + [C])

            for tile, v in ((src_i, 0), (dst_i, PAD_DST), (next_i, FAR), (etype_i, 0), (next_last, FAR), (after_next, FAR + 1)):
                dve.memset(tile[:, :], v).then_inc(cleared, 1)
            st.did(dve.memset(fix_idx[:, :], 16 * FAR))
            st.did(dve.memset(work[12][:, 0:ROW], 0.0))
            dve.memset(work[13][:, 0:D], 0.0).then_inc(default_ok, 1)
            st.wait()
            dve.memset(work[12][:, D + H:ROW], -LOW).then_inc(default_ok, 1)

            dve.wait_ge(tables_in, 16 * 10)
            st.did(dve.memset(cont[:, 0:1], 0.0))
            st.did(dve.tensor_tensor(cont[:, 1:ET], dst_i[:, 1:ET], dst_i[:, 0:ET - 1], ALU.is_equal))
            st.did(dve.tensor_scalar(xr_idx[:, :], dst_i[:, :], N - 1.0, None, ALU.min))
            st.did(dve.tensor_tensor(drop[:, :], dst_i[:, :], next_i[:, :], ALU.is_equal))
            st.did(dve.tensor_copy(last_f[:, :], dst_i[:, ET - 1:ET]))
            st.wait()
            st.did(dve.tensor_copy(flag[:, 0:1], drop[:, ET - 1:ET]))
            st.did(dve.scalar_tensor_tensor(out_idx[:, :], drop[:, :], float(FAR), dst_i[:, :], ALU.mult, ALU.add))
            st.did(dve.tensor_tensor(flag[:, 1:2], next_last[:, :], dst_i[:, ET - 1:ET], ALU.is_equal))
            st.did(dve.tensor_tensor(flag[:, 2:3], next_last[:, :], after_next[:, :], ALU.is_equal))
            st.wait()
            st.did(dve.tensor_scalar(drop[:, :], cont[:, :], 1.0, LOW, ALU.subtract, ALU.mult))
            st.did(dve.tensor_tensor(flag[:, 1:2], flag[:, 1:2], flag[:, 2:3], ALU.mult))
            st.wait()
            st.did(dve.tensor_scalar(flag[:, 2:3], flag[:, 1:2], -1.0, 1.0, ALU.mult, ALU.add))
            st.wait()
            st.did(dve.tensor_tensor(flag[:, 3:4], flag[:, 0:1], flag[:, 2:3], ALU.mult))
            st.wait()
            st.did(dve.tensor_scalar(flag[:, 2:3], flag[:, 3:4], -float(FAR), float(FAR), ALU.mult, ALU.add))
            st.wait()
            dve.tensor_tensor(fix_node[:, :], flag[:, 2:3], last_f[:, :], ALU.add).then_inc(tables_ok, 1)

            dve.wait_ge(weights_in, 16 * 11)

            def project(i, s, rows, tiles):
                after(dve, lr_out[s], 32 * i)
                for c, t0, n in chunks(tiles):
                    b = c % 2
                    dve.wait_ge(lr_ps[b], 4 * i + 2 * s + c // 2 + 1)
                    if n > 2:
                        dve.tensor_copy(lr[0:rows, s, t0 + 2:t0 + n, :].rearrange("p t d -> p (t d)"),
                                        psum[3 + 2 * b][0:rows, 0:(n - 2) * 256]).then_inc(r_cp[b], 1)
                    else:
                        dve.sem_inc(r_cp[b], 1)
                wait_group(dve, l_cp, i, s, tiles)
                wait_group(dve, r_cp, i, s, tiles)
                after(dve, l_read[1 - s], i + s)
                m_t = tiles_of(10)[0:rows, 0:tiles, :]
                st.did(dve.tensor_tensor(m_t, lr[0:rows, s, 0:tiles, 0:D], lr[0:rows, s, 0:tiles, D:2 * D], ALU.add))
                st.wait()
                st.did(dve.scalar_tensor_tensor(m_t, m_t, SLOPE, m_t, ALU.mult, ALU.max))
                st.wait()
                st.did(dve.tensor_tensor(m_t, m_t, over_tiles(att_b[0:rows, :], rows, tiles), ALU.mult))
                st.wait()
                at = bass.ds((2 * i + s) * NT, NT) if rows == P else slice(NG * NT, NG * NT + 1)
                dve.tensor_reduce(self_logit[0:rows, at, :], m_t.rearrange("p t (h c) -> p t h c", h=H),
                                  AX.X, ALU.add).then_inc(l_read[s], 1)

            node_groups(dve, project, st)
            end_stage(dve, 1)

            rows_of = lambda s: tiles_of(4 + s, EG, ROW)
            st.did(dve.memset(rows_of(1)[:, EG - 1, :], 0.0))
            st.wait()

            def attend(i, s):
                dve.wait_ge(at_in[s], 32 * EG * (i + 1))
                xs = tiles_of(s)[:, 0:EG, :]
                tmp = tiles_of(8)[:, 0:EG, :]
                R, before = rows_of(s), rows_of(1 - s)
                after(dve, at_row[1 - s], i + s)
                st.did(dve.tensor_tensor(tmp, xs, tiles_of(2 + s)[:, 0:EG, :], ALU.add))
                st.did(dve.tensor_copy(drop_st[:, s, :], drop[:, bass.ds((2 * i + s) * EG, EG)]))
                st.wait()
                st.did(dve.scalar_tensor_tensor(tmp, tmp, SLOPE, tmp, ALU.mult, ALU.max))
                st.wait()
                st.did(dve.tensor_tensor(tmp, tmp, over_tiles(att_b[:, :], P, EG), ALU.mult))
                st.wait()
                st.did(dve.tensor_reduce(logit[:, :, :], tmp.rearrange("p t (h c) -> p t h c", h=H), AX.X, ALU.add))
                st.wait()
                after(dve, at_out[s], 16 * i)
                for h in range(H):
                    st.did(dve.tensor_tensor_scan(R[:, :, D + H + h], drop_st[:, s, :], logit[:, :, h],
                                                  before[:, EG - 1, D + H + h:D + H + h + 1], ALU.add, ALU.max))
                st.wait()
                mx = R[:, :, D + H:ROW]
                st.did(dve.tensor_tensor(exp_in[:, 0, 0, :], before[:, EG - 1, D + H:ROW], mx[:, 0, :], ALU.subtract))
                st.did(dve.tensor_tensor(exp_in[:, 0, 1:EG, :], mx[:, 0:EG - 1, :], mx[:, 1:EG, :], ALU.subtract))
                st.did(dve.tensor_tensor(exp_in[:, 1, :, :], logit[:, :, :], mx, ALU.subtract))
                st.wait()
                dve.tensor_tensor(exp_in[:, 0, :, :], exp_in[:, 0, :, :],
                                  drop_st[:, s, :].unsqueeze(2).to_broadcast([P, EG, H]), ALU.add).then_inc(at_arg, 1)
                dve.wait_ge(at_exp, 2 * i + s + 1)
                fade, gain = exp_out[:, 0, :, :], exp_out[:, 1, :, :]
                val = tiles_of(9)[:, 0:EG, :]
                st.did(dve.tensor_tensor(val.rearrange("p t (h c) -> p t h c", h=H), xs.rearrange("p t (h c) -> p t h c", h=H),
                                         per_head(gain), ALU.mult))
                for h in range(H):
                    st.did(dve.tensor_tensor_scan(R[:, :, D + h], fade[:, :, h], gain[:, :, h],
                                                  before[:, EG - 1, D + h:D + h + 1], ALU.mult, ALU.add))
                st.wait()
                carried = work[10][:, 0:D]
                for t in range(EG):
                    prev = R[:, t - 1, 0:D] if t else before[:, EG - 1, 0:D]
                    st.did(dve.tensor_tensor(carried.rearrange("p (h c) -> p h c", h=H), prev.rearrange("p (h c) -> p h c", h=H),
                                             per_head(fade[:, t, :]), ALU.mult))
                    st.wait()
                    ins = dve.tensor_tensor(R[:, t, 0:D], carried, val[:, t, :], ALU.add)
                    if t < EG - 1:
                        st.did(ins)
                        st.wait()
                ins.then_inc(at_row[s], 1)

            def attend_pair(i):
                for s in range(2):
                    attend(i, s)
            in_pairs(dve, attend_pair, EITER, st)

            open_row = rows_of(1)[:, EG - 1, :]
            dve.wait_ge(at_row[1], EITER)
            dve.tensor_scalar(edge_m[:, 0, :], ident[:, :], last_f[:, 0:1], None, ALU.mult)
            dve.tensor_scalar(edge_m[:, 1, :], ident[:, :], flag[:, 0:1], None, ALU.mult)
            for h in range(H):
                last = dve.tensor_scalar(diag[:, h, :], ident[:, :], open_row[:, D + H + h:D + H + h + 1], None, ALU.mult)
            last.then_inc(fix_rd, 1)
            dve.memset(fix[:, :, :], 0.0).then_inc(fixed, 1)
            dve.wait_ge(fix_mm, 1)
            st.did(dve.tensor_scalar(edge_m[:, 2, :], psum[0][:, 0:P], last_f[:, 0:1], None, ALU.is_equal))
            st.wait()
            st.did(dve.tensor_scalar(edge_m[:, 0, :], edge_m[:, 2, :], flag[:, 0:1], None, ALU.mult))
            st.did(dve.tensor_tensor(edge_m[:, 2, :], edge_m[:, 2, :], psum[0][:, P:2 * P], ALU.mult))
            st.wait()
            st.did(dve.tensor_scalar(edge_m[:, 2, :], edge_m[:, 2, :], 1.0, LOW, ALU.subtract, ALU.mult))
            st.wait()
            st.did(dve.tensor_tensor(diag[:, :, :], psum[1][:, :].rearrange("p (h q) -> p h q", h=H),
                                     edge_m[:, 2, :].unsqueeze(1).to_broadcast([P, H, P]), ALU.add))
            st.wait()
            st.did(dve.tensor_reduce(fix_s[:, 0, :], diag[:, :, :], AX.X, ALU.max))
            st.wait()
            st.did(dve.tensor_tensor(fix_s[:, 1, :], open_row[:, D + H:ROW], fix_s[:, 0, :], ALU.subtract))
            st.wait()
            dve.tensor_scalar(fix_s[:, 1, :], fix_s[:, 1, :], 0.0, None, ALU.min).then_inc(fix_rd, 1)
            heads = lambda a: a.rearrange("p (h c) -> p h c", h=H)
            dve.wait_ge(fix_act, 1)
            dve.tensor_tensor(heads(work[10][:, 0:D]), heads(open_row[:, 0:D]), per_head(fix_s[:, 2, :]), ALU.mult)
            dve.tensor_tensor(work[10][:, D:D + H], open_row[:, D:D + H], fix_s[:, 2, :], ALU.mult).then_inc(fix_rd, 1)
            dve.wait_ge(fix_in, 16)
            st.did(dve.tensor_tensor(fix_s[:, 3, :], fix[:, 0, D + H:ROW], fix_s[:, 0, :], ALU.max))
            st.wait()
            dve.tensor_tensor(fix_s[:, 4, :], fix[:, 0, D + H:ROW], fix_s[:, 3, :], ALU.subtract)
            dve.tensor_tensor(fix_s[:, 5, :], fix_s[:, 0, :], fix_s[:, 3, :], ALU.subtract).then_inc(fix_rd, 1)
            dve.wait_ge(fix_act, 2)
            dve.wait_ge(fix_mm, 2)
            st.did(dve.tensor_tensor(heads(fix[:, 0, 0:D]), heads(fix[:, 0, 0:D]), per_head(fix_s[:, 6, :]), ALU.mult))
            st.did(dve.tensor_tensor(fix[:, 0, D:D + H], fix[:, 0, D:D + H], fix_s[:, 6, :], ALU.mult))
            st.did(dve.tensor_tensor(heads(fix[:, 1, 0:D]), heads(psum[2][:, 0:D]), per_head(fix_s[:, 7, :]), ALU.mult))
            st.did(dve.tensor_tensor(fix[:, 1, D:D + H], psum[2][:, D:D + H], fix_s[:, 7, :], ALU.mult))
            st.did(dve.tensor_copy(fix[:, 1, D + H:ROW], fix_s[:, 3, :]))
            st.wait()
            dve.tensor_tensor(fix[:, 1, 0:D + H], fix[:, 1, 0:D + H], fix[:, 0, 0:D + H], ALU.add).then_inc(fixed, 1)
            end_stage(dve, 2)

            dve.memset(work[12][:, 0:512], 0.0).then_inc(zeroed, 1)

            def merge_parts(i, s, rows, tiles):
                mx, den, tmp = (nsm[0:rows, k, 0:tiles, :] for k in range(3))
                return (tiles_of(s, NT, ROW)[0:rows, 0:tiles, :], mx, den, tmp,
                        nexp_in[0:rows, :, 0:tiles, :], nexp_out[0:rows, :, 0:tiles, :])

            def merge_args(i, s, rows, tiles):
                row, mx, den, tmp, e_in, e_out = merge_parts(i, s, rows, tiles)
                at = bass.ds((2 * i + s) * NT, NT) if rows == P else slice(NG * NT, NG * NT + 1)
                dve.wait_ge(ag_row[s], NODE_ROUND * i + 16 * tiles)
                own = self_logit[0:rows, at, :]
                st.did(dve.tensor_tensor(mx, row[:, :, D + H:ROW], own, ALU.max))
                st.wait()
                dve.tensor_tensor(e_in[:, 0], row[:, :, D + H:ROW], mx, ALU.subtract)
                dve.tensor_tensor(e_in[:, 1], own, mx, ALU.subtract).then_inc(ag_arg, 1)

            def merge_step(group, following):
                i, s, rows, tiles = group
                row, mx, den, tmp, e_in, e_out = merge_parts(*group)
                dve.wait_ge(ag_in[s], 16 * (i + 1))
                dve.wait_ge(ag_exp, 2 * i + s + 1)
                st.did(dve.tensor_tensor(den, row[:, :, D:D + H], e_out[:, 0], ALU.mult))
                st.wait()
                st.did(dve.scalar_tensor_tensor(den, den, 1e-16, e_out[:, 1], ALU.add, ALU.add))
                st.wait()
                st.did(dve.reciprocal(tmp, den))
                st.wait()
                for k in range(2):
                    st.did(dve.tensor_tensor(e_out[:, k], e_out[:, k], tmp, ALU.mult))
                st.wait()
                split = lambda a: a.rearrange("p t (h c) -> p t h c", h=H)
                part, own_part = tiles_of(9)[0:rows, 0:tiles, :], tiles_of(8)[0:rows, 0:tiles, :]
                dve.tensor_tensor(split(part), split(row[:, :, 0:D]), per_head(e_out[:, 0]), ALU.mult)
                dve.tensor_tensor(split(own_part), split(tiles_of(2 + s)[0:rows, 0:tiles, :]), per_head(e_out[:, 1]),
                                  ALU.mult).then_inc(ag_used[s], 1)
                dve.wait_ge(ag_used[s], i + 1)
                if following:
                    merge_args(*following)
                after(dve, cv_out[s], 16 * i)
                after(dve, cv_mm[s], i)
                dve.tensor_tensor(tiles_of(4 + s)[0:rows, 0:tiles, :], part, own_part, ALU.add).then_inc(cv_ok[s], 1)
                if s:
                    coefficients(i)
                else:
                    dve.wait_ge(cv_ok[s], i + 1)

            def coefficients(i):
                at = bass.ds(i * CT, CT)
                hot = work[11][:, 0:CT * RELS].rearrange("p (t r) -> p t r", r=RELS)
                st.did(dve.tensor_tensor(hot, etype_i[:, at].unsqueeze(2).to_broadcast([P, CT, RELS]),
                                         rel_id[:, :].unsqueeze(1).to_broadcast([P, CT, RELS]), ALU.is_equal))
                st.wait()
                for n in range(LAYERS * BASES // 2):
                    l, b = n * 2 // BASES, n * 2 % BASES
                    prod = work[(10, 13)[n % 2]][:, 0:2 * CT * RELS].rearrange("p (b t r) -> p b t r", b=2, r=RELS)
                    for k in range(2):
                        st.did(dve.tensor_tensor(prod[:, k], hot, comp_b[:, l, :, b + k].unsqueeze(1).to_broadcast([P, CT, RELS]), ALU.mult))
                    st.wait()
                    st.did(dve.tensor_reduce(coef[:, l, at, b:b + 2].rearrange("p t b -> p b t"), prod, AX.X, ALU.add))
                st.wait()

            node_steps(dve, merge_args, merge_step, st)

            dve.wait_ge(cv_mm[0], LAST + 1)
            dve.wait_ge(cv_mm[1], LAST)
            for b in range(2):
                st.did(dve.tensor_reduce(stat[:, b, :], psum[b][:, :].rearrange("p (k d) -> p d k", d=D), AX.X, ALU.add))
            st.wait()
            mean, sq, k_, d2, var = (stat[:, k, :] for k in range(5))
            st.did(dve.tensor_scalar(stat[:, 0:2, :], stat[:, 0:2, :], 1.0 / N, None, ALU.mult))
            st.wait()
            st.did(dve.tensor_tensor(k_, mean, conv_b[:, :], ALU.add))
            st.did(dve.tensor_tensor(d2, mean, mean, ALU.mult))
            st.wait()
            st.did(dve.tensor_tensor(k_, k_, gms_b[:, :], ALU.mult))
            st.did(dve.tensor_tensor(sq, sq, d2, ALU.subtract))
            st.wait()
            st.did(dve.tensor_tensor(k_, k_, conv_b[:, :], ALU.subtract))
            st.did(dve.tensor_scalar(sq, sq, 0.0, None, ALU.max))
            st.wait()
            st.did(dve.tensor_tensor(d2, mean, k_, ALU.subtract))
            st.wait()
            st.did(dve.tensor_tensor(d2, d2, d2, ALU.mult))
            st.wait()
            dve.scalar_tensor_tensor(var, d2, EPS, sq, ALU.add, ALU.add).then_inc(gn_var, 1)
            dve.wait_ge(gn_std, 1)
            st.did(dve.reciprocal(var, stat[:, 5, :]))
            st.wait()
            st.did(dve.tensor_tensor(gn_scale[:, :], var, gnw_b[:, :], ALU.mult))
            st.wait()
            st.did(dve.tensor_tensor(d2, k_, gn_scale[:, :], ALU.mult))
            st.wait()
            dve.tensor_tensor(gn_shift[:, :], gnb_b[:, :], d2, ALU.subtract).then_inc(gn_ok, 1)
            dve.wait_ge(gn_ok, 1)
            end_stage(dve, 3)

            def row_stats(z, rows, tiles, arg):
                for t in range(tiles):
                    ins = dve.bn_stats(bn6[0:rows, t, :], z[:, t, :])
                st.did(ins)
                st.wait()
                alone(dve)
                for t in range(tiles):
                    ins = dve.bn_aggr(bn2[0:rows, t, :], bn6[0:rows, t, :])
                st.did(ins)
                st.wait()
                dve.tensor_scalar(rstd[0:rows, 0, 0:tiles], bn2[0:rows, 0:tiles, 1], EPS, None, ALU.add).then_inc(arg, 1)

            def norm_rows(z, to, rows, tiles, done, count, free, ok):
                dve.wait_ge(done, count)
                st.did(dve.reciprocal(rstd[0:rows, 0, 0:tiles], rstd[0:rows, 1, 0:tiles]))
                st.wait()
                after(dve, *free)
                for t in range(tiles):
                    ins = dve.tensor_scalar(to[:, t, :], z[:, t, :], bn2[0:rows, t, 0:1], rstd[0:rows, 0, t:t + 1],
                                            ALU.subtract, ALU.mult)
                ins.then_inc(ok, 1)

            def scaled(i, s, rows, tiles):
                dve.wait_ge(nx_in[s], 32 * (i + 1))
                y = tiles_of(6)[0:rows, 0:tiles, :]
                st.did(dve.tensor_tensor(y, tiles_of(s)[0:rows, 0:tiles, :], over_tiles(gn_scale[0:rows, :], rows, tiles), ALU.mult))
                st.wait()
                dve.tensor_tensor(y, y, over_tiles(gn_shift[0:rows, :], rows, tiles), ALU.add).then_inc(nx_y, 1)

            def positive(i, s, rows, tiles):
                dve.wait_ge(nx_y, 2 * i + s + 1)
                dve.scalar_tensor_tensor(tiles_of(9)[0:rows, 0:tiles, :], tiles_of(6)[0:rows, 0:tiles, :], 0.0,
                                         tiles_of(2 + s)[0:rows, 0:tiles, :], ALU.max, ALU.add).then_inc(nx_used[s], 1)

            def first_norm(i, s, rows, tiles):
                scaled(i, s, rows, tiles)
                positive(i, s, rows, tiles)

            def norm_step(group, following):
                i, s, rows, tiles = group
                z = tiles_of(9)[0:rows, 0:tiles, :]
                dve.wait_ge(nx_used[s], i + 1)
                dve.wait_ge(nx_e, 2 * i + s + 1)
                st.did(dve.scalar_tensor_tensor(z, tiles_of(7)[0:rows, 0:tiles, :], -1.0, z, ALU.add, ALU.add))
                st.wait()
                row_stats(z, rows, tiles, nx_v)
                if following:
                    scaled(*following)
                norm_rows(z, tiles_of(4 + s)[0:rows, 0:tiles, :], rows, tiles, nx_r, 2 * i + s + 1,
                          (nx_out[s], 16 * i), nx_ok[s])
                if following:
                    dve.wait_ge(nx_ok[s], i + 1)
                    positive(*following)
            node_steps(dve, first_norm, norm_step, st)
            end_stage(dve, 4)

            for l in range(LAYERS):
                r = rel[l]
                rows_h = lambda s: tiles_of(4 + s)[:, 0:EG, :]
                st.did(dve.memset(rows_h(1)[:, EG - 1, :], 0.0))
                st.wait()

                def messages(i, s):
                    at = bass.ds((2 * i + s) * EG, EG)
                    st.did(dve.tensor_copy(coef_st[:, s, :, 0:BASES], coef[:, l, at, :]))
                    st.did(dve.tensor_copy(coef_st[:, s, :, BASES], cont[:, at]))
                    st.wait()
                    after(dve, r["out"][s], 16 * i)
                    marks = {}

                    def product(t, b):
                        y = psum[2 + (s * EG + t) % YBANKS][:, b * D:(b + 1) * D]
                        o, c = rows_h(s)[:, t, :], coef_st[:, s, t, b:b + 1]
                        tile = 2 * EG * i + s * EG + t + 1
                        if b == 0:
                            dve.wait_ge(r["y_ps"], tile)
                            ins = dve.tensor_scalar(o, y, c, None, ALU.mult)
                        else:
                            st.wait(marks[t, b - 1])
                            ins = dve.scalar_tensor_tensor(o, y, c, o, ALU.mult, ALU.add)
                        if b < BASES - 1:
                            st.did(ins)
                            marks[t, b] = st.n
                        else:
                            ins.then_inc(r["y_used"], 1)

                    def run_sum(t):
                        o = rows_h(s)[:, t, :]
                        prev = rows_h(s)[:, t - 1, :] if t else rows_h(1 - s)[:, EG - 1, :]
                        dve.wait_ge(r["y_used"], 2 * EG * i + s * EG + t + 1)
                        if t:
                            st.wait(marks[t - 1])
                        else:
                            after(dve, r["row"][1 - s], i + s)
                        ins = dve.scalar_tensor_tensor(o, prev, coef_st[:, s, t, BASES:BASES + 1], o, ALU.mult, ALU.add)
                        if t < EG - 1:
                            st.did(ins)
                            marks[t] = st.n
                        else:
                            ins.then_inc(r["row"][s], 1)

                    for t in range(-1, EG + 1):
                        if t + 1 < EG:
                            product(t + 1, 0)
                        if 0 <= t < EG:
                            product(t, 2)
                        if t >= 1:
                            run_sum(t - 1)
                        if t + 1 < EG:
                            product(t + 1, 1)
                        if 0 <= t < EG:
                            product(t, 3)
                def message_pair(i):
                    messages(i, 0)
                    messages(i, 1)
                in_pairs(dve, message_pair, EITER, st)
                dve.wait_ge(fix_in, 16 * (2 + l))
                dve.wait_ge(fix_mm, 3 + l)
                dve.tensor_tensor(fix[:, 1, 0:D], fix[:, 0, 0:D], psum[0][:, 0:D], ALU.add).then_inc(fixed, 1)
                end_stage(dve, 5 + 2 * l)

                def update(i, s, rows, tiles):
                    dve.wait_ge(r["n_row"][s], NODE_ROUND * i + 16 * tiles)
                    after(dve, r["nh_ok" if l == 0 else "h_ok"][s], i)
                    for c, t0, n in chunks(tiles):
                        b = c % 2
                        dve.wait_ge(r["nm_ps"][b], 4 * i + 2 * s + c // 2 + 1)
                        dve.tensor_tensor(work[10 + s][0:rows, t0 * D:(t0 + n) * D], psum[2 + b][0:rows, 0:n * D],
                                          work[s][0:rows, t0 * D:(t0 + n) * D], ALU.add).then_inc(r["nm_used"][b], 1)
                    wait_group(dve, r["nm_used"], i, s, tiles)
                    dve.sem_inc(r["s_ok"][s], 1)

                def update_step(group, following):
                    i, s, rows, tiles = group
                    z = tiles_of(12 + s)[0:rows, 0:tiles, :]
                    dve.wait_ge(r["n_in"][s], 32 * (i + 1))
                    dve.wait_ge(r["h_ok"][s], i + 1)
                    dve.tensor_tensor(z, z, tiles_of(4 + s)[0:rows, 0:tiles, :], ALU.add).then_inc(r["z_ok"][s], 1)
                    dve.wait_ge(r["z_ok"][s], i + 1)
                    row_stats(z, rows, tiles, r["v_ok"])
                    if following:
                        update(*following)
                    norm_rows(z, tiles_of(6 + s)[0:rows, 0:tiles, :], rows, tiles, r["r_ok"], 2 * i + s + 1,
                              (r["nh_out"][s], 16 * i), r["nh_ok"][s])
                if l == 0:
                    node_groups(dve, update, st)
                else:
                    node_steps(dve, update, update_step, st)
                end_stage(dve, 6 + 2 * l)


_INS = ['x', 'src', 'dst', 'edge_type_32', 'L0_gnn_Wl', 'L0_gnn_Wr', 'L0_gnn_att', 'L0_gnn_bias_conv',
        'L0_gnn_gn_weight', 'L0_gnn_gn_bias', 'L0_gnn_gn_mean_scale', 'L1_gnn_basis', 'L1_gnn_comp',
        'L1_gnn_loop_w', 'L1_gnn_bias']


def kernel(**inputs):
    import numpy as _np
    import concourse.bacc as _bacc
    from concourse import mybir as _mybir
    from concourse.bass_utils import run_bass_kernel_spmd as _run

    nc = _bacc.Bacc("TRN2", target_bir_lowering=False, num_devices=1)
    arrays, args = {}, []
    for name in _INS:
        a = _np.ascontiguousarray(inputs[name])
        arrays[f"in_{name}_dram"] = a
        args.append(nc.dram_tensor(f"in_{name}_dram", a.shape, _mybir.dt.from_np(a.dtype), kind="ExternalInput").ap())
    args.append(nc.dram_tensor("out_0_dram", (N, D), _mybir.dt.float32, kind="ExternalOutput").ap())
    gnn_kernel(nc, *args)
    r = _run(nc, [arrays], core_ids=[0])
    return r.results[0]["out_0_dram"]
```

```python
from contextlib import ExitStack

import concourse.bass as bass
from concourse import mybir

F32 = mybir.dt.float32
I32 = mybir.dt.int32
ALU = mybir.AluOpType
ACT = mybir.ActivationFunctionType
AX = mybir.AxisListType

P = 128
D = 128
H = 4
C = D // H
BASES = 4
RELS = 32
LAYERS = 2
N = 50000
E = 50000

NT = 13
GROUP = NT * P
NG = N // GROUP
TAIL = N - NG * GROUP
LAST = NG // 2
NODE_TILES = NG * NT + 1

ET = 392
EG = 7
EGROUPS = ET // EG
EITER = EGROUPS // 2
FULL_E = (P - 1) * ET
REST_E = E - FULL_E

EPAD = P * ET
CT = -(-ET // NG)
NODE_ROUND = 16 * NT

ROW = D + 2 * H
FAR = 65536
PAD_DST = 65535
LOW = 1e30
SLOPE = 0.2
EPS = 1e-5


def chunks(tiles):
    return [(c, t, min(4, tiles - t)) for c, t in enumerate(range(0, tiles, 4))]


def after(eng, sem, count):
    if not isinstance(count, int) or count > 0:
        eng.wait_ge(sem, count)


def wait_group(eng, bank_sems, i, s, tiles):
    eng.wait_ge(bank_sems[0], 4 * i + 2 * s + (2 if tiles > 8 else 1))
    if tiles > 4:
        eng.wait_ge(bank_sems[1], 4 * i + 2 * s + (2 if tiles > 12 else 1))


YBANKS = 5
EDGE_CHUNKS = [(0, 0, 4), (1, 4, EG - 4)]


class Steps:

    def __init__(self, eng, sem):
        self.eng, self.sem, self.base, self.n, self.turns, self.per = eng, sem, 0, 0, None, 0

    def enter(self, turns, per):
        self.base, self.n, self.turns, self.per = self.base + self.n, 0, turns, per

    def leave(self, rounds):
        assert self.n == self.per, (self.n, self.per)
        self.base, self.n, self.turns = self.base + self.per * rounds, 0, None

    def did(self, ins):
        ins.then_inc(self.sem, 1)
        self.n += 1

    def wait(self, upto=None):
        at = self.base + (self.n if upto is None else upto)
        self.eng.wait_ge(self.sem, at if self.turns is None else self.turns * self.per + at)


def in_pairs(eng, pair, rounds, steps=None):
    before = steps.n if steps else 0
    pair(0)
    per = steps.n - before if steps else 0
    with eng.Fori(1, rounds) as i:
        if steps:
            steps.enter(i - 1, per)
        pair(i)
    if steps:
        steps.leave(rounds - 1)


def node_groups(eng, body, steps=None):
    def pair(i):
        body(i, 0, P, NT)
        body(i, 1, P, NT)
    in_pairs(eng, pair, LAST, steps)
    body(LAST, 0, TAIL, 1)


def node_steps(eng, first, step, steps=None):
    def pair(i):
        step((i, 0, P, NT), (i, 1, P, NT))
        step((i, 1, P, NT), (i + 1, 0, P, NT))
    first(0, 0, P, NT)
    in_pairs(eng, pair, LAST - 1, steps)
    step((LAST - 1, 0, P, NT), (LAST - 1, 1, P, NT))
    step((LAST - 1, 1, P, NT), (LAST, 0, TAIL, 1))
    step((LAST, 0, TAIL, 1), None)


def node_rows(dram, i, s, rows, tiles):
    if rows == P:
        part = dram[bass.ds((2 * i + s) * GROUP, GROUP), :]
    else:
        part = dram[NG * GROUP:N, :]
    return part.rearrange("(p t) d -> p (t d)", t=tiles)


def gnn_kernel(nc, x, src, dst, etype, Wl, Wr, att, bias_conv, gn_weight, gn_bias, gn_mean_scale,
               basis, comp, loop_w, bias, out):
    ctx = ExitStack()
    with ctx:
        def sb(name, shape, dt=F32):
            return ctx.enter_context(nc.sbuf_tensor(name, shape, dt))

        def sem(name):
            return ctx.enter_context(nc.semaphore(name))

        def sems(name):
            return [sem(f"{name}{k}") for k in range(2)]

        xl_d = nc.dram_tensor("xl_d", [N, D], F32).ap()
        xr_d = nc.dram_tensor("xr_d", [N, D], F32).ap()
        gat_d = nc.dram_tensor("gat_d", [EPAD + P, ROW], F32).ap()
        conv_d = nc.dram_tensor("conv_d", [N, D], F32).ap()
        x1_d = nc.dram_tensor("x1_d", [N, D], F32).ap()
        agg_d = nc.dram_tensor("agg_d", [EPAD + P, D], F32).ap()
        last_d = nc.dram_tensor("last_d", [N, 1], I32).ap()
        h1_d = nc.dram_tensor("h1_d", [N, D], F32).ap()

        pad_d = nc.dram_tensor("pad_d", [EPAD], I32).ap()
        sorted_d = [nc.dram_tensor(f"sorted_{n}_d", [E, 1], I32).ap() for n in ("src", "dst", "etype")]

        src_i = sb("src_i", [P, ET], I32)
        dst_i = sb("dst_i", [P, ET], I32)
        next_i = sb("next_i", [P, ET], I32)
        etype_i = sb("etype_i", [P, CT * NG], I32)
        edge_id = sb("edge_id", [P, ET], I32)
        no_edge = sb("no_edge", [P, NG * NT], I32)
        node_idx = sb("node_idx", [P, NODE_TILES], I32)
        xr_idx = sb("xr_idx", [P, ET], I32)
        out_idx = sb("out_idx", [P, ET], I32)
        cont = sb("cont", [P, ET])
        drop = sb("drop", [P, ET])
        coef = sb("coef", [P, LAYERS, CT * NG, BASES])
        self_logit = sb("self_logit", [P, NODE_TILES, H])
        ident = sb("ident", [P, P])
        ones = sb("ones", [P, P])
        w_lr = sb("w_lr", [D, 2 * D])
        att_b = sb("att_b", [P, D])
        conv_b = sb("conv_b", [P, D])
        gnw_b = sb("gnw_b", [P, D])
        gnb_b = sb("gnb_b", [P, D])
        gms_b = sb("gms_b", [P, D])
        bias_b = sb("bias_b", [P, LAYERS, D])
        comp_b = sb("comp_b", [P, LAYERS, RELS, BASES])
        basis_s = sb("basis_s", [D, LAYERS, BASES, D])
        loop_s = sb("loop_s", [D, LAYERS, D])
        rel_id = sb("rel_id", [P, RELS])
        gn_scale = sb("gn_scale", [P, D])
        gn_shift = sb("gn_shift", [P, D])
        stat = sb("stat", [P, 6, D])
        next_last = sb("next_last", [P, 1], I32)
        after_next = sb("after_next", [P, 1], I32)
        last_f = sb("last_f", [P, 1])
        flag = sb("flag", [P, 4])
        unsorted = sb("unsorted", [P, 2])
        unsorted_i = sb("unsorted_i", [P, 1], I32)
        fix_node = sb("fix_node", [P, 1], I32)
        fix_idx = sb("fix_idx", [P, 1], I32)
        edge_m = sb("edge_m", [P, 3, P])
        fix = sb("fix", [P, 2, ROW])
        fix_s = sb("fix_s", [P, 8, H])
        diag = sb("diag", [P, H, P])
        idx_st = sb("idx_st", [P, 2, 2, EG], I32)
        node_st = sb("node_st", [P, 2, NT], I32)
        drop_st = sb("drop_st", [P, 2, EG])
        coef_st = sb("coef_st", [P, 2, EG, BASES + 1])
        logit = sb("logit", [P, EG, H])
        exp_in = sb("exp_in", [P, 2, EG, H])
        exp_out = sb("exp_out", [P, 2, EG, H])
        nexp_in = sb("nexp_in", [P, 2, NT, H])
        nexp_out = sb("nexp_out", [P, 2, NT, H])
        nsm = sb("nsm", [P, 3, NT, H])
        bn6 = sb("bn6", [P, NT, 6])
        bn2 = sb("bn2", [P, NT, 2])
        rstd = sb("rstd", [P, 2, NT])
        affine = sb("affine", [P, 2, 2, NT])
        work = [sb(f"work{k}", [P, NT * ROW]) for k in range(14)]

        lr = sb("lr", [P, 2, NT, 2 * D])

        def tiles_of(k, tiles=NT, width=D):
            return work[k][:, 0:tiles * width].rearrange("p (t d) -> p t d", d=width)

        psum = [ctx.enter_context(nc.psum_tensor(f"bank{k}", [P, 512], F32)) for k in range(8)]

        cleared = sem("cleared")
        tables_in = sem("tables_in")
        weights_in = sem("weights_in")
        consts = sem("consts")
        tables_ok = sem("tables_ok")
        order_seen, order_all, order_known = sem("order_seen"), sem("order_all"), sem("order_known")
        row_in, row_used, places_ok, moved, sorted_in = (
            sem("row_in"), sem("row_used"), sem("places_ok"), sem("moved"), sem("sorted_in"))
        filled = sem("filled")
        default_ok = sem("default_ok")
        last_out = sems("last_out")
        node_idx_in = sem("node_idx_in")
        fix_idx_in = sem("fix_idx_in")
        stage_done = sem("stage_done")
        passed = sem("passed")
        dve_steps = sem("dve_steps")
        pool_steps = sem("pool_steps")
        act_steps = sem("act_steps")

        x_in, x_used = sems("x_in"), sems("x_used")
        xt_ps, xt_cp = sems("xt_ps"), sems("xt_cp")
        lr_ps, l_cp, r_cp, l_read, lr_out = sems("lr_ps"), sems("l_cp"), sems("r_cp"), sems("l_read"), sems("lr_out")
        at_in, at_row, at_out = sems("at_in"), sems("at_row"), sems("at_out")
        at_arg, at_exp = sem("at_arg"), sem("at_exp")
        fix_rd, fix_mm, fix_act, fix_in, fix_out, fixed = (
            sem("fix_rd"), sem("fix_mm"), sem("fix_act"), sem("fix_in"), sem("fix_out"), sem("fixed"))
        ag_in, ag_used, cv_ok, cv_sq, cv_mm, cv_out = (
            sems("ag_in"), sems("ag_used"), sems("cv_ok"), sems("cv_sq"), sems("cv_mm"), sems("cv_out"))
        ag_arg, ag_exp, ag_row = sem("ag_arg"), sem("ag_exp"), sems("ag_row")
        zeroed, gn_var, gn_std, gn_ok = sem("zeroed"), sem("gn_var"), sem("gn_std"), sem("gn_ok")
        nx_in, nx_used, nx_ok, nx_out = sems("nx_in"), sems("nx_used"), sems("nx_ok"), sems("nx_out")
        nx_y, nx_e, nx_v, nx_r, nx_n = sem("nx_y"), sem("nx_e"), sem("nx_v"), sem("nx_r"), sem("nx_n")
        rel = []
        for l in range(LAYERS):
            rel.append({n: sems(f"r{l}_{n}") for n in (
                "h_in", "t_ps", "t_cp", "row", "out",
                "n_in", "n_row", "nt_ps", "nt_cp", "nm_ps", "nm_used", "s_ok", "nh_ok", "nh_out",
                ) + (("h_ok", "z_ok") if l else ())} | {n: sem(f"r{l}_{n}") for n in (("v_ok", "r_ok") if l else ())})
        y_ps, y_used, coef_ok, first_ok = sem("y_ps"), sem("y_used"), sem("coef_ok"), sem("first_ok")

        def alone(eng):
            eng.sem_inc(passed, 1)

        def end_stage(eng, k):
            eng.drain().then_inc(stage_done, 1)
            eng.wait_ge(stage_done, 5 * k)

        def if_unsorted(eng):
            eng.wait_ge(order_known, 1)
            return eng.If(eng.value_load(unsorted_i[0:1, 0:1]) > 0)

        block = ctx.enter_context(nc.Block())

        edge_rows = lambda a, o=0: a[o:o + FULL_E].rearrange("(p t) -> p t", t=ET)

        @block.sync
        def _(sp):
            sp.dma_start(w_lr[:, 0:D], Wl).then_inc(weights_in, 16)
            sp.dma_start(w_lr[:, D:2 * D], Wr).then_inc(weights_in, 16)
            for tile, row in ((att_b[:, :], att.rearrange("h c -> (h c)")), (conv_b[:, :], bias_conv),
                              (gnw_b[:, :], gn_weight), (gnb_b[:, :], gn_bias), (gms_b[:, :], gn_mean_scale),
                              (bias_b[:, :, :].rearrange("p l d -> p (l d)"), bias.rearrange("l d -> (l d)")),
                              (comp_b[:, :, :, :].rearrange("p l r b -> p (l r b)"),
                               comp.rearrange("l r b -> (l r b)"))):
                sp.dma_start(tile, row.partition_broadcast(P)).then_inc(weights_in, 16)
            sp.dma_start(basis_s[:, :, :, :], basis.rearrange("l b k n -> k l b n")).then_inc(weights_in, 16)
            sp.dma_start(loop_s[:, :, :], loop_w.rearrange("l k n -> k l n")).then_inc(weights_in, 16)
            sp.wait_ge(cleared, 6)
            def load_tables(src_a, dst_a, etype_a, into):
                for tile, a, o in ((src_i, src_a, 0), (dst_i, dst_a, 0), (etype_i, etype_a, 0), (next_i, dst_a, 1)):
                    sp.dma_start(tile[0:P - 1, 0:ET], edge_rows(a, o)).then_inc(into, 16)
                    sp.dma_start(tile[P - 1:P, 0:REST_E - o],
                                 a[FULL_E + o:E].rearrange("(p t) -> p t", p=1)).then_inc(into, 16)
                sp.dma_start(next_last[0:P - 2, :], edge_rows(dst_a)[1:P - 1, ET - 1:ET],
                             allow_slow_non_contiguous=True).then_inc(into, 16)
                sp.dma_start(after_next[0:P - 2, :], dst_a[ET + 1:ET + 1 + (P - 2) * ET]
                             .rearrange("(p t) -> p t", t=ET)[:, ET - 1:ET],
                             allow_slow_non_contiguous=True).then_inc(into, 16)
            load_tables(src, dst, etype, tables_in)

            sp.wait_ge(default_ok, 2)
            sp.dma_start(gat_d[EPAD:EPAD + P, :], work[12][:, 0:ROW]).then_inc(filled, 16)
            sp.dma_start(agg_d[EPAD:EPAD + P, :], work[13][:, 0:D]).then_inc(filled, 16)
            sp.wait_ge(consts, 5)
            sp.dma_start(last_d[0:NG * GROUP, :].rearrange("(p t) o -> p (t o)", p=P), no_edge[:, :]).then_inc(filled, 16)
            sp.dma_start(last_d[NG * GROUP:N, :], no_edge[0:TAIL, 0:1]).then_inc(filled, 16)

            with if_unsorted(sp):
                sp.dma_start(pad_d.rearrange("(p t) -> p t", t=ET), dst_i[:, :]).then_inc(sorted_in, 16)
                sp.wait_ge(sorted_in, 16)

                def show_row(q):
                    after(sp, row_used, q)
                    sp.dma_start(out_idx[:, :], pad_d[bass.ds(q * ET, ET)].partition_broadcast(P)).then_inc(row_in, 16)
                in_pairs(sp, show_row, P)
                sp.wait_ge(moved, 16 * 3 * ET)
                load_tables(*(a.rearrange("e o -> (e o)") for a in sorted_d), sorted_in)

            def stream(load, store):
                def pair(i):
                    for s in range(2):
                        load(i + 1, s, P, NT)
                        store(i, s, P, NT)
                for s in range(2):
                    load(0, s, P, NT)
                in_pairs(sp, pair, LAST - 1)
                load(LAST, 0, TAIL, 1)
                for s in range(2):
                    store(LAST - 1, s, P, NT)
                store(LAST, 0, TAIL, 1)

            def load(dram, k, into, i, s, rows, tiles):
                sp.dma_start(work[k + s][0:rows, 0:tiles * D], node_rows(dram, i, s, rows, tiles)).then_inc(into[s], 16)

            def save(dram, k, done, i, s, rows, tiles):
                sp.dma_start(node_rows(dram, i, s, rows, tiles), work[k + s][0:rows, 0:tiles * D]).then_inc(done[s], 16)

            def stored(done, each=16):
                sp.wait_ge(done[0], each * (LAST + 1))
                sp.wait_ge(done[1], each * LAST)

            def load_x(i, s, rows, tiles):
                after(sp, x_used[s], i)
                load(x, 0, x_in, i, s, rows, tiles)

            def save_lr(i, s, rows, tiles):
                wait_group(sp, r_cp, i, s, tiles)
                wait_group(sp, l_cp, i, s, tiles)
                for k, dram in enumerate((xl_d, xr_d)):
                    sp.dma_start(node_rows(dram, i, s, rows, tiles).rearrange("p (t d) -> p t d", d=D),
                                 lr[0:rows, s, 0:tiles, k * D:(k + 1) * D]).then_inc(lr_out[s], 16)
            stream(load_x, save_lr)
            stored(lr_out, 32)
            end_stage(sp, 1)

            sp.dma_start(node_idx[:, 0:NG * NT].rearrange("p (g t) -> p g t", t=NT),
                         last_d[0:NG * GROUP, :].rearrange("(g p t) o -> p g (t o)", p=P, t=NT)).then_inc(node_idx_in, 16)
            sp.dma_start(node_idx[0:TAIL, NG * NT:NODE_TILES], last_d[NG * GROUP:N, :]).then_inc(node_idx_in, 16)
            sp.wait_ge(node_idx_in, 32)

            def save_rows(dram, k, width, ready, done):
                by_edge = dram[0:EPAD, :].rearrange("(p t) d -> p t d", t=ET)

                def pair(i):
                    for s in range(2):
                        sp.wait_ge(ready[s], i + 1)
                        sp.dma_start(by_edge[:, bass.ds((2 * i + s) * EG, EG), :].rearrange("p t d -> p (t d)"),
                                     work[k + s][:, 0:EG * width]).then_inc(done[s], 16)
                in_pairs(sp, pair, EITER)
                for s in range(2):
                    sp.wait_ge(done[s], 16 * EITER)
            save_rows(gat_d, 4, ROW, at_row, at_out)
            sp.wait_ge(fix_out, 16)
            end_stage(sp, 2)

            def load_xl(i, s, rows, tiles):
                after(sp, ag_used[s], i)
                load(xl_d, 2, ag_in, i, s, rows, tiles)

            def save_cv(i, s, rows, tiles):
                sp.wait_ge(cv_ok[s], i + 1)
                save(conv_d, 4, cv_out, i, s, rows, tiles)
            stream(load_xl, save_cv)
            stored(cv_out)
            end_stage(sp, 3)

            def load_nx(i, s, rows, tiles):
                after(sp, nx_used[s], i)
                load(conv_d, 0, nx_in, i, s, rows, tiles)
                load(x, 2, nx_in, i, s, rows, tiles)

            def save_nx(i, s, rows, tiles):
                sp.wait_ge(nx_ok[s], i + 1)
                save(x1_d, 4, nx_out, i, s, rows, tiles)
            stream(load_nx, save_nx)
            stored(nx_out)
            end_stage(sp, 4)

            for l in range(LAYERS):
                r = rel[l]
                save_rows(agg_d, 4, D, r["row"], r["out"])
                sp.wait_ge(fix_out, 16 * (2 + l))
                end_stage(sp, 5 + 2 * l)

                def load_n(i, s, rows, tiles):
                    after(sp, r["s_ok" if l == 0 else "z_ok"][s], i)
                    load((x1_d, h1_d)[l], 2, r["n_in"], i, s, rows, tiles)
                    if l == LAYERS - 1:
                        load(x1_d, 4, r["n_in"], i, s, rows, tiles)

                def save_n(i, s, rows, tiles):
                    sp.wait_ge(r["nh_ok"][s], i + 1)
                    save((h1_d, out)[l], 6, r["nh_out"], i, s, rows, tiles)
                stream(load_n, save_n)
                stored(r["nh_out"])
                end_stage(sp, 6 + 2 * l)

        @block.gpsimd
        def _(pool):
            st = Steps(pool, pool_steps)
            pool.iota(rel_id[:, :], [[1, RELS]], base=0, channel_multiplier=0,
                      allow_small_or_imprecise_dtypes=True).then_inc(consts, 1)
            st.did(pool.memset(ident[:, :], 0.0))
            st.wait()
            pool.affine_select(out=ident[:, :], in_=ident[:, :], compare_op=ALU.not_equal, fill=1.0,
                               base=0, pattern=[[-1, P]], channel_multiplier=1).then_inc(consts, 1)
            pool.memset(ones[:, :], 1.0).then_inc(consts, 1)

            st.did(pool.iota(edge_id[:, :], [[1, ET]], base=0, channel_multiplier=ET))
            pool.iota(no_edge[:, :], [[0, NG * NT]], base=EPAD, channel_multiplier=1).then_inc(consts, 1)
            pool.sem_inc(consts, 1)

            def stage_idx(k, table, i, s):
                st.did(pool.tensor_copy(idx_st[:, s, k, :], table[:, bass.ds((2 * i + s) * EG, EG)]))

            def column(s, k, t):
                return bass.IndirectOffsetOnAxis(ap=idx_st[:, s, k, t:t + 1], axis=0)

            pool.wait_ge(order_seen, 1)
            pool.partition_all_reduce(unsorted[:, 1:2], unsorted[:, 0:1], P, bass.bass_isa.ReduceOp.max).then_inc(order_all, 1)
            with if_unsorted(pool):
                pool.wait_ge(places_ok, 1)
                for k, (table, dram) in enumerate(zip((src_i, dst_i, etype_i), sorted_d)):
                    def move(g):
                        after(pool, moved, 16 * (k * ET + g * EG))
                        at = bass.ds(g * EG, EG)
                        pool.tensor_copy(idx_st[:, 0, 0, :], xr_idx[:, at])
                        pool.tensor_copy(idx_st[:, 0, 1, :], table[:, at])
                        pool.drain()
                        alone(pool)
                        for t in range(EG):
                            pool.indirect_dma_start(dram, column(0, 0, t), idx_st[:, 0, 1, t:t + 1], None,
                                                    bounds_check=E - 1, oob_is_err=False).then_inc(moved, 16)
                    in_pairs(pool, move, EGROUPS)
                pool.wait_ge(moved, 16 * 3 * ET)

            pool.wait_ge(tables_ok, 1)
            pool.wait_ge(filled, 16 * 4)

            def last_edges(i):
                for s in range(2):
                    after(pool, last_out[s], 16 * EG * i)
                    stage_idx(0, out_idx, i, s)
                    stage_idx(1, edge_id, i, s)
                    st.wait()
                    alone(pool)
                    for t in range(EG):
                        pool.indirect_dma_start(last_d, column(s, 0, t), idx_st[:, s, 1, t:t + 1], None,
                                                bounds_check=N - 1, oob_is_err=False).then_inc(last_out[s], 16)
            in_pairs(pool, last_edges, EITER, st)
            for s in range(2):
                pool.wait_ge(last_out[s], 16 * EG * EITER)
            pool.indirect_dma_start(fix_idx[:, :], None, last_d, bass.IndirectOffsetOnAxis(ap=fix_node[:, 0:1], axis=0),
                                    bounds_check=N - 1, oob_is_err=False).then_inc(fix_idx_in, 16)
            pool.wait_ge(fix_idx_in, 16)
            end_stage(pool, 1)

            def gather_at(i):
                for s in range(2):
                    after(pool, at_row[s], i)
                    stage_idx(0, src_i, i, s)
                    stage_idx(1, xr_idx, i, s)
                    st.wait()
                    alone(pool)
                    for t in range(EG):
                        for k, dram in enumerate((xl_d, xr_d)):
                            pool.indirect_dma_start(tiles_of(2 * k + s)[:, t, :], None, dram, column(s, k, t)).then_inc(at_in[s], 16)
            in_pairs(pool, gather_at, EITER, st)
            by_fix = bass.IndirectOffsetOnAxis(ap=fix_idx[:, 0:1], axis=0)
            for s in range(2):
                pool.wait_ge(at_out[s], 16 * EITER)
            pool.wait_ge(fixed, 1)
            pool.indirect_dma_start(fix[:, 0, :], None, gat_d, by_fix, bounds_check=EPAD - 1, oob_is_err=False).then_inc(fix_in, 16)
            pool.wait_ge(fixed, 2)
            pool.indirect_dma_start(gat_d, by_fix, fix[:, 1, :], None, bounds_check=EPAD - 1, oob_is_err=False).then_inc(fix_out, 16)
            pool.wait_ge(fix_out, 16)
            end_stage(pool, 2)

            def gather_nodes(dram, width, free, into):
                def group(i, s, rows, tiles):
                    after(pool, free[s], i)
                    at = bass.ds((2 * i + s) * NT, NT) if rows == P else slice(NG * NT, NODE_TILES)
                    st.did(pool.tensor_copy(node_st[0:rows, s, 0:tiles], node_idx[0:rows, at]))
                    st.wait()
                    alone(pool)
                    for t in range(tiles):
                        pool.indirect_dma_start(tiles_of(s, NT, width)[0:rows, t, :], None, dram,
                                                bass.IndirectOffsetOnAxis(ap=node_st[0:rows, s, t:t + 1], axis=0)).then_inc(into[s], 16)
                node_groups(pool, group, st)
            gather_nodes(gat_d, ROW, ag_used, ag_row)
            end_stage(pool, 3)
            end_stage(pool, 4)

            for l in range(LAYERS):
                r = rel[l]

                def gather_h(i):
                    for s in range(2):
                        after(pool, r["t_ps"][1], 2 * i + s - 1)
                        stage_idx(0, src_i, i, s)
                        st.wait()
                        alone(pool)
                        for t in range(EG):
                            pool.indirect_dma_start(tiles_of(s)[:, t, :], None, (x1_d, h1_d)[l], column(s, 0, t)).then_inc(r["h_in"][s], 16)
                in_pairs(pool, gather_h, EITER, st)
                for s in range(2):
                    pool.wait_ge(r["out"][s], 16 * EITER)
                pool.indirect_dma_start(fix[:, 0, 0:D], None, agg_d, by_fix, bounds_check=EPAD - 1, oob_is_err=False).then_inc(fix_in, 16)
                pool.wait_ge(fixed, 3 + l)
                pool.indirect_dma_start(agg_d, by_fix, fix[:, 1, 0:D], None, bounds_check=EPAD - 1, oob_is_err=False).then_inc(fix_out, 16)
                pool.wait_ge(fix_out, 16 * (2 + l))
                end_stage(pool, 5 + 2 * l)
                gather_nodes(agg_d, D, r["s_ok"], r["n_row"])
                end_stage(pool, 6 + 2 * l)

        @block.tensor
        def _(pe):
            pe.wait_ge(consts, 3)
            pe.wait_ge(weights_in, 16 * 11)

            def transpose_chunk(tiles, rows, c, t0, n, use, ps, cp):
                after(pe, cp[c % 2], use)
                for t in range(t0, t0 + n):
                    last = pe.transpose(psum[c % 2][:, (t - t0) * P:(t - t0) * P + rows],
                                        tiles[0:rows, t, :], ident[0:rows, 0:rows])
                last.then_inc(ps[c % 2], 1)

            def project(i, s, rows, tiles):
                pe.wait_ge(x_in[s], 16 * (i + 1))
                todo = chunks(tiles)

                def multiply(c, t0, n):
                    use = 4 * i + 2 * s + c // 2
                    b = c % 2
                    pe.wait_ge(xt_cp[b], use + 1)
                    after(pe, l_cp[b], use)
                    after(pe, r_cp[b], use)
                    for t in range(t0, t0 + n):
                        k = t - t0
                        last = pe.matmul(psum[2 + 2 * b + k // 2][0:rows, (k % 2) * 256:(k % 2) * 256 + 256],
                                         tiles_of(8 + s)[:, t, 0:rows], w_lr[:, :], start=True, stop=True)
                        if c == len(todo) - 2 and k == 0:
                            last.then_inc(x_used[s], 1)
                    last.then_inc(lr_ps[b], 1)

                for c, t0, n in todo:
                    transpose_chunk(tiles_of(s), rows, c, t0, n, 4 * i + 2 * s + c // 2, xt_ps, xt_cp)
                    if c:
                        multiply(*todo[c - 1])
                multiply(*todo[-1])
            node_groups(pe, project)
            end_stage(pe, 1)

            pe.wait_ge(fix_rd, 1)
            pe.matmul(psum[0][:, 0:P], ones[:, :], edge_m[:, 0, :], start=True, stop=True)
            pe.matmul(psum[0][:, P:2 * P], ones[:, :], edge_m[:, 1, :], start=True, stop=True)
            pe.matmul(psum[1][:, :], ones[:, :], diag[:, :, :].rearrange("p h q -> p (h q)"), start=True, stop=True).then_inc(fix_mm, 1)
            pe.wait_ge(fix_rd, 3)
            pe.matmul(psum[2][:, 0:D + H], edge_m[:, 0, :], work[10][:, 0:D + H], start=True, stop=True).then_inc(fix_mm, 1)
            end_stage(pe, 2)

            pe.wait_ge(zeroed, 1)
            for b in range(2):
                pe.matmul(psum[b][:, :], ones[:, :], work[12][:, 0:512], start=True, stop=False, skip_group_check=True)

            def sums(i, s, rows, tiles):
                for b, (sig, k) in enumerate(((cv_ok, 4), (cv_sq, 6))):
                    pe.wait_ge(sig[s], i + 1)
                    for c, t0, n in chunks(tiles):
                        last = pe.matmul(psum[b][:, 0:n * D], ones[0:rows, :],
                                         work[k + s][0:rows, t0 * D:(t0 + n) * D], start=False, stop=False,
                                         skip_group_check=True)
                last.then_inc(cv_mm[s], 1)
            node_groups(pe, sums)
            end_stage(pe, 3)
            end_stage(pe, 4)

            for l in range(LAYERS):
                r = rel[l]

                def turn(i, s):
                    pe.wait_ge(r["h_in"][s], 16 * EG * (i + 1))
                    for c, t0, n in EDGE_CHUNKS:
                        after(pe, r["t_cp"][c], 2 * i + s)
                        for t in range(t0, t0 + n):
                            last = pe.transpose(psum[c][:, (t - t0) * P:(t - t0 + 1) * P], tiles_of(s)[:, t, :], ident[:, :])
                        last.then_inc(r["t_ps"][c], 1)

                def expand(i, s):
                    for c, t0, n in EDGE_CHUNKS:
                        pe.wait_ge(r["t_cp"][c], 2 * i + s + 1)
                        for t in range(t0, t0 + n):
                            k = s * EG + t
                            user = 2 * EG * i + k - YBANKS if k >= YBANKS else (
                                2 * EG * (i - 1) + max(q for q in range(2 * EG) if q % YBANKS == k))
                            after(pe, y_used, l * ET + user + 1)
                            pe.matmul(psum[2 + k % YBANKS][:, :], tiles_of(2 + s)[:, t, :],
                                      basis_s[:, l, :, :].rearrange("k b n -> k (b n)"), start=True, stop=True).then_inc(y_ps, 1)

                def edge_pair(i):
                    turn(i, 1)
                    expand(i, 0)
                    turn(i + 1, 0)
                    expand(i, 1)
                turn(0, 0)
                in_pairs(pe, edge_pair, EITER - 1)
                turn(EITER - 1, 1)
                expand(EITER - 1, 0)
                expand(EITER - 1, 1)
                pe.wait_ge(r["row"][1], EITER)
                pe.matmul(psum[0][:, 0:D], edge_m[:, 0, :], tiles_of(5)[:, EG - 1, :], start=True, stop=True).then_inc(fix_mm, 1)
                end_stage(pe, 5 + 2 * l)

                def nodes(i, s, rows, tiles):
                    pe.wait_ge(r["n_in"][s], (16 + 16 * l) * (i + 1))
                    todo = chunks(tiles)

                    def multiply(c, t0, n):
                        use, b = 4 * i + 2 * s + c // 2, c % 2
                        pe.wait_ge(r["nt_cp"][b], use + 1)
                        after(pe, r["nm_used"][b], use - 1)
                        pe.matmul(psum[2 + c][0:rows, 0:n * D], ones[0:1, 0:rows],
                                  bias_b[0:1, l, :].unsqueeze(1).to_broadcast([1, n, D]), start=True, stop=False)
                        for t in range(t0, t0 + n):
                            last = pe.matmul(psum[2 + c][0:rows, (t - t0) * D:(t - t0 + 1) * D],
                                             tiles_of(8 + s)[:, t, 0:rows], loop_s[:, l, :],
                                             start=False, stop=(t == t0 + n - 1))
                        last.then_inc(r["nm_ps"][b], 1)

                    for c, t0, n in todo:
                        transpose_chunk(tiles_of(2 + s), rows, c, t0, n, 4 * i + 2 * s + c // 2, r["nt_ps"], r["nt_cp"])
                        if c:
                            multiply(*todo[c - 1])
                    multiply(*todo[-1])
                node_groups(pe, nodes)
                end_stage(pe, 6 + 2 * l)

        @block.scalar
        def _(act):
            st = Steps(act, act_steps)

            def copy_turned(i, s, rows, n, c, t0, k, ps, cp):
                act.wait_ge(ps[c % 2], 4 * i + 2 * s + c // 2 + 1)
                act.activation(tiles_of(k + s)[:, t0:t0 + n, 0:rows],
                               psum[c % 2][:, 0:n * P].rearrange("p (t d) -> p t d", d=P)[:, :, 0:rows],
                               ACT.Copy).then_inc(cp[c % 2], 1)

            def project(i, s, rows, tiles):
                todo = chunks(tiles)
                after(act, lr_out[s], 32 * i)
                after(act, l_read[s], i)

                def copy_l(c, t0, n):
                    b, m = c % 2, min(2, n)
                    act.wait_ge(lr_ps[b], 4 * i + 2 * s + c // 2 + 1)
                    act.activation(lr[0:rows, s, t0:t0 + m, :].rearrange("p t d -> p (t d)"),
                                   psum[2 + 2 * b][0:rows, 0:m * 256], ACT.Copy).then_inc(l_cp[b], 1)
                for c, t0, n in todo:
                    copy_turned(i, s, rows, n, c, t0, 8, xt_ps, xt_cp)
                    if c:
                        copy_l(*todo[c - 1])
                copy_l(*todo[-1])
            node_groups(act, project)
            end_stage(act, 1)

            with act.Fori(0, EGROUPS) as g:
                act.wait_ge(at_arg, g + 1)
                act.activation(exp_out[:, :, :, :], exp_in[:, :, :, :], ACT.Exp).then_inc(at_exp, 1)
            act.wait_ge(fix_rd, 2)
            act.activation(fix_s[:, 2, :], fix_s[:, 1, :], ACT.Exp).then_inc(fix_act, 1)
            act.wait_ge(fix_rd, 4)
            act.activation(fix_s[:, 6:8, :], fix_s[:, 4:6, :], ACT.Exp).then_inc(fix_act, 1)
            end_stage(act, 2)

            def exps(i, s, rows, tiles):
                act.wait_ge(ag_arg, 2 * i + s + 1)
                act.activation(nexp_out[0:rows, :, 0:tiles, :], nexp_in[0:rows, :, 0:tiles, :], ACT.Exp).then_inc(ag_exp, 1)

            def squares(group, following):
                i, s, rows, tiles = group
                if following:
                    exps(*following)
                act.wait_ge(cv_ok[s], i + 1)
                after(act, cv_mm[s], i)
                act.activation(work[6 + s][0:rows, 0:tiles * D], work[4 + s][0:rows, 0:tiles * D], ACT.Square).then_inc(cv_sq[s], 1)
            node_steps(act, exps, squares)
            act.wait_ge(gn_var, 1)
            act.activation(stat[:, 5, :], stat[:, 4, :], ACT.Sqrt).then_inc(gn_std, 1)
            end_stage(act, 3)

            def elu_part(i, s, rows, tiles):
                act.wait_ge(nx_y, 2 * i + s + 1)
                w = tiles * D
                st.did(act.activation(work[8][0:rows, 0:w], work[6][0:rows, 0:w], ACT.Relu, scale=-1.0))
                st.wait()
                act.activation(work[7][0:rows, 0:w], work[8][0:rows, 0:w], ACT.Exp, scale=-1.0).then_inc(nx_e, 1)

            def deviation(group, arg, done):
                i, s, rows, tiles = group
                act.wait_ge(arg, 2 * i + s + 1)
                act.activation(rstd[0:rows, 1, 0:tiles], rstd[0:rows, 0, 0:tiles], ACT.Sqrt).then_inc(done, 1)

            def elu_step(group, following):
                i, s, rows, tiles = group
                deviation(group, nx_v, nx_r)
                if following:
                    elu_part(*following)
                act.wait_ge(nx_n, 2 * i + s + 1)
                after(act, nx_out[s], 16 * i)
                for t in range(tiles):
                    ins = act.activation(tiles_of(4 + s)[0:rows, t, :], tiles_of(9 + s)[0:rows, t, :], ACT.Identity,
                                         bias=affine[0:rows, s, 1, t:t + 1], scale=affine[0:rows, s, 0, t:t + 1])
                ins.then_inc(nx_ok[s], 1)
            node_steps(act, elu_part, elu_step, st)
            end_stage(act, 4)

            for l in range(LAYERS):
                r = rel[l]

                def turned(i, s):
                    for c, t0, n in EDGE_CHUNKS:
                        act.wait_ge(r["t_ps"][c], 2 * i + s + 1)
                        act.activation(tiles_of(2 + s)[:, t0:t0 + n, :],
                                       psum[c][:, 0:n * P].rearrange("p (t d) -> p t d", d=P),
                                       ACT.Copy).then_inc(r["t_cp"][c], 1)
                def first_terms(i, s):
                    act.wait_ge(coef_ok, l * EGROUPS + 2 * i + s + 1)
                    after(act, r["out"][s], 16 * i)
                    for t in range(EG):
                        k = s * EG + t
                        act.wait_ge(y_ps, l * ET + 2 * EG * i + k + 1)
                        act.activation(tiles_of(4 + s)[:, t, :], psum[2 + k % YBANKS][:, 0:D], ACT.Copy,
                                       scale=coef_st[:, s, t, 0:1]).then_inc(first_ok, 1)

                def edge_pair(i):
                    turned(i, 1)
                    first_terms(i, 0)
                    turned(i + 1, 0)
                    first_terms(i, 1)
                turned(0, 0)
                in_pairs(act, edge_pair, EITER - 1)
                turned(EITER - 1, 1)
                first_terms(EITER - 1, 0)
                first_terms(EITER - 1, 1)
                end_stage(act, 5 + 2 * l)

                def copies(i, s, rows, tiles):
                    for c, t0, n in chunks(tiles):
                        copy_turned(i, s, rows, n, c, t0, 8, r["nt_ps"], r["nt_cp"])

                def finish(i, s, rows, tiles):
                    act.wait_ge(r["s_ok"][s], i + 1)
                    if l == 0:
                        after(act, r["nh_out"][s], 16 * i)
                        to, done = work[6 + s], r["nh_ok"]
                    else:
                        after(act, r["nh_ok"][s], i)
                        to, done = work[12 + s], r["h_ok"]
                    act.activation(to[0:rows, 0:tiles * D], work[10 + s][0:rows, 0:tiles * D], ACT.Tanh).then_inc(done[s], 1)

                def nodes(*group):
                    copies(*group)
                    finish(*group)

                def node_step(group, following):
                    if following:
                        copies(*following)
                    deviation(group, r["v_ok"], r["r_ok"])
                    if following:
                        finish(*following)
                if l == 0:
                    node_groups(act, nodes)
                else:
                    node_steps(act, nodes, node_step)
                end_stage(act, 6 + 2 * l)

        @block.vector
        def _(dve):
            st = Steps(dve, dve_steps)

            def over_tiles(row, rows, tiles):
                return row.unsqueeze(1).to_broadcast([rows, tiles, D])

            def per_head(small):
                a = small.unsqueeze(len(small.shape))
                return a.to_broadcast(list(small.shape) + [C])

            for tile, v in ((src_i, 0), (dst_i, PAD_DST), (next_i, FAR), (etype_i, 0), (next_last, FAR), (after_next, FAR + 1)):
                dve.memset(tile[:, :], v).then_inc(cleared, 1)
            st.did(dve.memset(fix_idx[:, :], 16 * FAR))
            st.did(dve.memset(work[12][:, 0:ROW], 0.0))
            dve.memset(work[13][:, 0:D], 0.0).then_inc(default_ok, 1)
            st.wait()
            dve.memset(work[12][:, D + H:ROW], -LOW).then_inc(default_ok, 1)

            dve.wait_ge(tables_in, 16 * 10)
            backward = work[0][:, 0:ET]
            st.did(dve.tensor_tensor(backward, next_i[:, :], dst_i[:, :], ALU.is_lt))
            st.wait()
            dve.tensor_reduce(unsorted[:, 0:1], backward, AX.X, ALU.max).then_inc(order_seen, 1)
            dve.wait_ge(order_all, 1)
            dve.tensor_copy(unsorted_i[:, :], unsorted[:, 1:2]).then_inc(order_known, 1)
            with if_unsorted(dve):
                dst_f, pos, row_f, bound = (work[k][:, 0:ET] for k in range(1, 5))
                shifted = work[5]
                first_id, row_id, part = (fix_s[:, k, 0:1] for k in range(3))
                hits = work[6][:, 0:4 * ET].rearrange("p (j k) -> p j k", k=ET)
                dve.wait_ge(consts, 5)
                dve.tensor_copy(dst_f, dst_i[:, :])
                dve.tensor_copy(shifted[:, ET:2 * ET], dst_i[:, :])
                dve.memset(shifted[:, 0:ET], -1.0)
                dve.memset(pos, 0.0)
                dve.memset(row_id, 0.0)
                dve.tensor_copy(first_id, edge_id[:, 0:1])
                dve.drain()
                with dve.Fori(0, P) as q:
                    dve.wait_ge(row_in, 16 * (q + 1))
                    dve.tensor_copy(row_f, out_idx[:, :]).then_inc(row_used, 1)
                    dve.tensor_tensor(part, first_id, row_id, ALU.is_gt)
                    dve.drain()
                    dve.tensor_scalar(part, part, 0.5, None, ALU.mult)
                    dve.tensor_scalar(row_id, row_id, float(ET), None, ALU.add)
                    dve.drain()
                    dve.tensor_scalar(bound, dst_f, part, None, ALU.add)
                    dve.drain()
                    with dve.Fori(0, ET // 4) as c:
                        at = bass.ds(c * 4, 4)
                        dve.tensor_tensor(hits, row_f.unsqueeze(1).to_broadcast([P, 4, ET]),
                                          bound[:, at].unsqueeze(2).to_broadcast([P, 4, ET]), ALU.is_lt)
                        dve.drain()
                        dve.tensor_reduce(fix_s[:, 3, :], hits, AX.X, ALU.add)
                        dve.drain()
                        dve.tensor_tensor(pos[:, at], pos[:, at], fix_s[:, 3, :], ALU.add)
                        dve.drain()
                with dve.Fori(0, ET - 1) as c:
                    dve.tensor_tensor(row_f, shifted[:, bass.ds(c + 1, ET)], shifted[:, ET:2 * ET], ALU.is_equal)
                    dve.drain()
                    dve.tensor_tensor(pos, pos, row_f, ALU.add)
                    dve.drain()
                dve.tensor_copy(xr_idx[:, :], pos).then_inc(places_ok, 1)
                dve.wait_ge(sorted_in, 16 * 11)
            st.did(dve.memset(cont[:, 0:1], 0.0))
            st.did(dve.tensor_tensor(cont[:, 1:ET], dst_i[:, 1:ET], dst_i[:, 0:ET - 1], ALU.is_equal))
            st.did(dve.tensor_scalar(xr_idx[:, :], dst_i[:, :], N - 1.0, None, ALU.min))
            st.did(dve.tensor_tensor(drop[:, :], dst_i[:, :], next_i[:, :], ALU.is_equal))
            st.did(dve.tensor_copy(last_f[:, :], dst_i[:, ET - 1:ET]))
            st.wait()
            st.did(dve.tensor_copy(flag[:, 0:1], drop[:, ET - 1:ET]))
            st.did(dve.scalar_tensor_tensor(out_idx[:, :], drop[:, :], float(FAR), dst_i[:, :], ALU.mult, ALU.add))
            st.did(dve.tensor_tensor(flag[:, 1:2], next_last[:, :], dst_i[:, ET - 1:ET], ALU.is_equal))
            st.did(dve.tensor_tensor(flag[:, 2:3], next_last[:, :], after_next[:, :], ALU.is_equal))
            st.wait()
            st.did(dve.tensor_scalar(drop[:, :], cont[:, :], 1.0, LOW, ALU.subtract, ALU.mult))
            st.did(dve.tensor_tensor(flag[:, 1:2], flag[:, 1:2], flag[:, 2:3], ALU.mult))
            st.wait()
            st.did(dve.tensor_scalar(flag[:, 2:3], flag[:, 1:2], -1.0, 1.0, ALU.mult, ALU.add))
            st.wait()
            st.did(dve.tensor_tensor(flag[:, 3:4], flag[:, 0:1], flag[:, 2:3], ALU.mult))
            st.wait()
            st.did(dve.tensor_scalar(flag[:, 2:3], flag[:, 3:4], -float(FAR), float(FAR), ALU.mult, ALU.add))
            st.wait()
            dve.tensor_tensor(fix_node[:, :], flag[:, 2:3], last_f[:, :], ALU.add).then_inc(tables_ok, 1)

            def coefficients(l, at, tiles, spare):
                hot = work[spare[0]][:, 0:tiles * RELS].rearrange("p (t r) -> p t r", r=RELS)
                prods = [work[spare[1 + k]][:, 0:2 * tiles * RELS].rearrange("p (b t r) -> p b t r", b=2, r=RELS)
                         for k in range(2)]
                st.did(dve.tensor_tensor(hot, etype_i[:, at].unsqueeze(2).to_broadcast([P, tiles, RELS]),
                                         rel_id[:, :].unsqueeze(1).to_broadcast([P, tiles, RELS]), ALU.is_equal))
                st.wait()
                for b in range(BASES):
                    st.did(dve.tensor_tensor(prods[b // 2][:, b % 2], hot,
                                             comp_b[:, l, :, b].unsqueeze(1).to_broadcast([P, tiles, RELS]), ALU.mult))
                st.wait()
                for b in (0, 2):
                    st.did(dve.tensor_reduce(coef[:, l, at, b:b + 2].rearrange("p t b -> p b t"), prods[b // 2], AX.X, ALU.add))
                st.wait()

            dve.wait_ge(weights_in, 16 * 11)
            dve.wait_ge(consts, 5)

            def project(i, s, rows, tiles):
                after(dve, lr_out[s], 32 * i)
                for c, t0, n in chunks(tiles):
                    b = c % 2
                    dve.wait_ge(lr_ps[b], 4 * i + 2 * s + c // 2 + 1)
                    if n > 2:
                        dve.tensor_copy(lr[0:rows, s, t0 + 2:t0 + n, :].rearrange("p t d -> p (t d)"),
                                        psum[3 + 2 * b][0:rows, 0:(n - 2) * 256]).then_inc(r_cp[b], 1)
                    else:
                        dve.sem_inc(r_cp[b], 1)
                wait_group(dve, l_cp, i, s, tiles)
                wait_group(dve, r_cp, i, s, tiles)
                after(dve, l_read[1 - s], i + s)
                m_t = tiles_of(10)[0:rows, 0:tiles, :]
                st.did(dve.tensor_tensor(m_t, lr[0:rows, s, 0:tiles, 0:D], lr[0:rows, s, 0:tiles, D:2 * D], ALU.add))
                st.wait()
                st.did(dve.scalar_tensor_tensor(m_t, m_t, SLOPE, m_t, ALU.mult, ALU.max))
                st.wait()
                st.did(dve.tensor_tensor(m_t, m_t, over_tiles(att_b[0:rows, :], rows, tiles), ALU.mult))
                st.wait()
                at = bass.ds((2 * i + s) * NT, NT) if rows == P else slice(NG * NT, NG * NT + 1)
                dve.tensor_reduce(self_logit[0:rows, at, :], m_t.rearrange("p t (h c) -> p t h c", h=H),
                                  AX.X, ALU.add).then_inc(l_read[s], 1)

            node_groups(dve, project, st)
            end_stage(dve, 1)

            rows_of = lambda s: tiles_of(4 + s, EG, ROW)
            st.did(dve.memset(rows_of(1)[:, EG - 1, :], 0.0))
            st.wait()

            def attend(i, s):
                dve.wait_ge(at_in[s], 32 * EG * (i + 1))
                xs = tiles_of(s)[:, 0:EG, :]
                tmp = tiles_of(8)[:, 0:EG, :]
                R, before = rows_of(s), rows_of(1 - s)
                after(dve, at_row[1 - s], i + s)
                st.did(dve.tensor_tensor(tmp, xs, tiles_of(2 + s)[:, 0:EG, :], ALU.add))
                st.did(dve.tensor_copy(drop_st[:, s, :], drop[:, bass.ds((2 * i + s) * EG, EG)]))
                st.wait()
                st.did(dve.scalar_tensor_tensor(tmp, tmp, SLOPE, tmp, ALU.mult, ALU.max))
                st.wait()
                st.did(dve.tensor_tensor(tmp, tmp, over_tiles(att_b[:, :], P, EG), ALU.mult))
                st.wait()
                st.did(dve.tensor_reduce(logit[:, :, :], tmp.rearrange("p t (h c) -> p t h c", h=H), AX.X, ALU.add))
                st.wait()
                after(dve, at_out[s], 16 * i)
                for h in range(H):
                    st.did(dve.tensor_tensor_scan(R[:, :, D + H + h], drop_st[:, s, :], logit[:, :, h],
                                                  before[:, EG - 1, D + H + h:D + H + h + 1], ALU.add, ALU.max))
                st.wait()
                mx = R[:, :, D + H:ROW]
                st.did(dve.tensor_tensor(exp_in[:, 0, 0, :], before[:, EG - 1, D + H:ROW], mx[:, 0, :], ALU.subtract))
                st.did(dve.tensor_tensor(exp_in[:, 0, 1:EG, :], mx[:, 0:EG - 1, :], mx[:, 1:EG, :], ALU.subtract))
                st.did(dve.tensor_tensor(exp_in[:, 1, :, :], logit[:, :, :], mx, ALU.subtract))
                st.wait()
                dve.tensor_tensor(exp_in[:, 0, :, :], exp_in[:, 0, :, :],
                                  drop_st[:, s, :].unsqueeze(2).to_broadcast([P, EG, H]), ALU.add).then_inc(at_arg, 1)
                dve.wait_ge(at_exp, 2 * i + s + 1)
                fade, gain = exp_out[:, 0, :, :], exp_out[:, 1, :, :]
                val = tiles_of(9)[:, 0:EG, :]
                st.did(dve.tensor_tensor(val.rearrange("p t (h c) -> p t h c", h=H), xs.rearrange("p t (h c) -> p t h c", h=H),
                                         per_head(gain), ALU.mult))
                for h in range(H):
                    st.did(dve.tensor_tensor_scan(R[:, :, D + h], fade[:, :, h], gain[:, :, h],
                                                  before[:, EG - 1, D + h:D + h + 1], ALU.mult, ALU.add))
                st.wait()
                carried = work[10][:, 0:D]
                for t in range(EG):
                    prev = R[:, t - 1, 0:D] if t else before[:, EG - 1, 0:D]
                    st.did(dve.tensor_tensor(carried.rearrange("p (h c) -> p h c", h=H), prev.rearrange("p (h c) -> p h c", h=H),
                                             per_head(fade[:, t, :]), ALU.mult))
                    st.wait()
                    ins = dve.tensor_tensor(R[:, t, 0:D], carried, val[:, t, :], ALU.add)
                    if t < EG - 1:
                        st.did(ins)
                        st.wait()
                ins.then_inc(at_row[s], 1)

            def attend_pair(i):
                for s in range(2):
                    attend(i, s)
                    coefficients(0, bass.ds((2 * i + s) * EG, EG), EG, (11, 12, 13))
            in_pairs(dve, attend_pair, EITER, st)

            open_row = rows_of(1)[:, EG - 1, :]
            dve.wait_ge(at_row[1], EITER)
            dve.tensor_scalar(edge_m[:, 0, :], ident[:, :], last_f[:, 0:1], None, ALU.mult)
            dve.tensor_scalar(edge_m[:, 1, :], ident[:, :], flag[:, 0:1], None, ALU.mult)
            for h in range(H):
                last = dve.tensor_scalar(diag[:, h, :], ident[:, :], open_row[:, D + H + h:D + H + h + 1], None, ALU.mult)
            last.then_inc(fix_rd, 1)
            dve.memset(fix[:, :, :], 0.0).then_inc(fixed, 1)
            dve.wait_ge(fix_mm, 1)
            st.did(dve.tensor_scalar(edge_m[:, 2, :], psum[0][:, 0:P], last_f[:, 0:1], None, ALU.is_equal))
            st.wait()
            st.did(dve.tensor_scalar(edge_m[:, 0, :], edge_m[:, 2, :], flag[:, 0:1], None, ALU.mult))
            st.did(dve.tensor_tensor(edge_m[:, 2, :], edge_m[:, 2, :], psum[0][:, P:2 * P], ALU.mult))
            st.wait()
            st.did(dve.tensor_scalar(edge_m[:, 2, :], edge_m[:, 2, :], 1.0, LOW, ALU.subtract, ALU.mult))
            st.wait()
            st.did(dve.tensor_tensor(diag[:, :, :], psum[1][:, :].rearrange("p (h q) -> p h q", h=H),
                                     edge_m[:, 2, :].unsqueeze(1).to_broadcast([P, H, P]), ALU.add))
            st.wait()
            st.did(dve.tensor_reduce(fix_s[:, 0, :], diag[:, :, :], AX.X, ALU.max))
            st.wait()
            st.did(dve.tensor_tensor(fix_s[:, 1, :], open_row[:, D + H:ROW], fix_s[:, 0, :], ALU.subtract))
            st.wait()
            dve.tensor_scalar(fix_s[:, 1, :], fix_s[:, 1, :], 0.0, None, ALU.min).then_inc(fix_rd, 1)
            heads = lambda a: a.rearrange("p (h c) -> p h c", h=H)
            dve.wait_ge(fix_act, 1)
            dve.tensor_tensor(heads(work[10][:, 0:D]), heads(open_row[:, 0:D]), per_head(fix_s[:, 2, :]), ALU.mult)
            dve.tensor_tensor(work[10][:, D:D + H], open_row[:, D:D + H], fix_s[:, 2, :], ALU.mult).then_inc(fix_rd, 1)
            dve.wait_ge(fix_in, 16)
            st.did(dve.tensor_tensor(fix_s[:, 3, :], fix[:, 0, D + H:ROW], fix_s[:, 0, :], ALU.max))
            st.wait()
            dve.tensor_tensor(fix_s[:, 4, :], fix[:, 0, D + H:ROW], fix_s[:, 3, :], ALU.subtract)
            dve.tensor_tensor(fix_s[:, 5, :], fix_s[:, 0, :], fix_s[:, 3, :], ALU.subtract).then_inc(fix_rd, 1)
            dve.wait_ge(fix_act, 2)
            dve.wait_ge(fix_mm, 2)
            st.did(dve.tensor_tensor(heads(fix[:, 0, 0:D]), heads(fix[:, 0, 0:D]), per_head(fix_s[:, 6, :]), ALU.mult))
            st.did(dve.tensor_tensor(fix[:, 0, D:D + H], fix[:, 0, D:D + H], fix_s[:, 6, :], ALU.mult))
            st.did(dve.tensor_tensor(heads(fix[:, 1, 0:D]), heads(psum[2][:, 0:D]), per_head(fix_s[:, 7, :]), ALU.mult))
            st.did(dve.tensor_tensor(fix[:, 1, D:D + H], psum[2][:, D:D + H], fix_s[:, 7, :], ALU.mult))
            st.did(dve.tensor_copy(fix[:, 1, D + H:ROW], fix_s[:, 3, :]))
            st.wait()
            dve.tensor_tensor(fix[:, 1, 0:D + H], fix[:, 1, 0:D + H], fix[:, 0, 0:D + H], ALU.add).then_inc(fixed, 1)
            end_stage(dve, 2)

            dve.memset(work[12][:, 0:512], 0.0).then_inc(zeroed, 1)

            def merge_parts(i, s, rows, tiles):
                mx, den, tmp = (nsm[0:rows, k, 0:tiles, :] for k in range(3))
                return (tiles_of(s, NT, ROW)[0:rows, 0:tiles, :], mx, den, tmp,
                        nexp_in[0:rows, :, 0:tiles, :], nexp_out[0:rows, :, 0:tiles, :])

            def merge_args(i, s, rows, tiles):
                row, mx, den, tmp, e_in, e_out = merge_parts(i, s, rows, tiles)
                at = bass.ds((2 * i + s) * NT, NT) if rows == P else slice(NG * NT, NG * NT + 1)
                dve.wait_ge(ag_row[s], NODE_ROUND * i + 16 * tiles)
                own = self_logit[0:rows, at, :]
                st.did(dve.tensor_tensor(mx, row[:, :, D + H:ROW], own, ALU.max))
                st.wait()
                dve.tensor_tensor(e_in[:, 0], row[:, :, D + H:ROW], mx, ALU.subtract)
                dve.tensor_tensor(e_in[:, 1], own, mx, ALU.subtract).then_inc(ag_arg, 1)

            def merge_step(group, following):
                i, s, rows, tiles = group
                row, mx, den, tmp, e_in, e_out = merge_parts(*group)
                dve.wait_ge(ag_in[s], 16 * (i + 1))
                dve.wait_ge(ag_exp, 2 * i + s + 1)
                st.did(dve.tensor_tensor(den, row[:, :, D:D + H], e_out[:, 0], ALU.mult))
                st.wait()
                st.did(dve.scalar_tensor_tensor(den, den, 1e-16, e_out[:, 1], ALU.add, ALU.add))
                st.wait()
                st.did(dve.reciprocal(tmp, den))
                st.wait()
                for k in range(2):
                    st.did(dve.tensor_tensor(e_out[:, k], e_out[:, k], tmp, ALU.mult))
                st.wait()
                split = lambda a: a.rearrange("p t (h c) -> p t h c", h=H)
                part, own_part = tiles_of(9)[0:rows, 0:tiles, :], tiles_of(8)[0:rows, 0:tiles, :]
                dve.tensor_tensor(split(part), split(row[:, :, 0:D]), per_head(e_out[:, 0]), ALU.mult)
                dve.tensor_tensor(split(own_part), split(tiles_of(2 + s)[0:rows, 0:tiles, :]), per_head(e_out[:, 1]),
                                  ALU.mult).then_inc(ag_used[s], 1)
                dve.wait_ge(ag_used[s], i + 1)
                if following:
                    merge_args(*following)
                after(dve, cv_out[s], 16 * i)
                after(dve, cv_mm[s], i)
                dve.tensor_tensor(tiles_of(4 + s)[0:rows, 0:tiles, :], part, own_part, ALU.add).then_inc(cv_ok[s], 1)
                dve.wait_ge(cv_ok[s], i + 1)
            node_steps(dve, merge_args, merge_step, st)

            dve.wait_ge(cv_mm[0], LAST + 1)
            dve.wait_ge(cv_mm[1], LAST)
            for b in range(2):
                st.did(dve.tensor_reduce(stat[:, b, :], psum[b][:, :].rearrange("p (k d) -> p d k", d=D), AX.X, ALU.add))
            st.wait()
            mean, sq, k_, d2, var = (stat[:, k, :] for k in range(5))
            st.did(dve.tensor_scalar(stat[:, 0:2, :], stat[:, 0:2, :], 1.0 / N, None, ALU.mult))
            st.wait()
            st.did(dve.tensor_tensor(k_, mean, conv_b[:, :], ALU.add))
            st.did(dve.tensor_tensor(d2, mean, mean, ALU.mult))
            st.wait()
            st.did(dve.tensor_tensor(k_, k_, gms_b[:, :], ALU.mult))
            st.did(dve.tensor_tensor(sq, sq, d2, ALU.subtract))
            st.wait()
            st.did(dve.tensor_tensor(k_, k_, conv_b[:, :], ALU.subtract))
            st.did(dve.tensor_scalar(sq, sq, 0.0, None, ALU.max))
            st.wait()
            st.did(dve.tensor_tensor(d2, mean, k_, ALU.subtract))
            st.wait()
            st.did(dve.tensor_tensor(d2, d2, d2, ALU.mult))
            st.wait()
            dve.scalar_tensor_tensor(var, d2, EPS, sq, ALU.add, ALU.add).then_inc(gn_var, 1)
            dve.wait_ge(gn_std, 1)
            st.did(dve.reciprocal(var, stat[:, 5, :]))
            st.wait()
            st.did(dve.tensor_tensor(gn_scale[:, :], var, gnw_b[:, :], ALU.mult))
            st.wait()
            st.did(dve.tensor_tensor(d2, k_, gn_scale[:, :], ALU.mult))
            st.wait()
            dve.tensor_tensor(gn_shift[:, :], gnb_b[:, :], d2, ALU.subtract).then_inc(gn_ok, 1)
            dve.wait_ge(gn_ok, 1)
            end_stage(dve, 3)

            def row_stats(z, rows, tiles, arg):
                for t in range(tiles):
                    ins = dve.bn_stats(bn6[0:rows, t, :], z[:, t, :])
                st.did(ins)
                st.wait()
                alone(dve)
                for t in range(tiles):
                    ins = dve.bn_aggr(bn2[0:rows, t, :], bn6[0:rows, t, :])
                st.did(ins)
                st.wait()
                dve.tensor_scalar(rstd[0:rows, 0, 0:tiles], bn2[0:rows, 0:tiles, 1], EPS, None, ALU.add).then_inc(arg, 1)

            def norm_rows(z, to, rows, tiles, done, count, free, ok):
                dve.wait_ge(done, count)
                st.did(dve.reciprocal(rstd[0:rows, 0, 0:tiles], rstd[0:rows, 1, 0:tiles]))
                st.wait()
                after(dve, *free)
                for t in range(tiles):
                    ins = dve.tensor_scalar(to[:, t, :], z[:, t, :], bn2[0:rows, t, 0:1], rstd[0:rows, 0, t:t + 1],
                                            ALU.subtract, ALU.mult)
                ins.then_inc(ok, 1)

            def scaled(i, s, rows, tiles):
                dve.wait_ge(nx_in[s], 32 * (i + 1))
                y = tiles_of(6)[0:rows, 0:tiles, :]
                st.did(dve.tensor_tensor(y, tiles_of(s)[0:rows, 0:tiles, :], over_tiles(gn_scale[0:rows, :], rows, tiles), ALU.mult))
                st.wait()
                dve.tensor_tensor(y, y, over_tiles(gn_shift[0:rows, :], rows, tiles), ALU.add).then_inc(nx_y, 1)

            def positive(i, s, rows, tiles):
                dve.wait_ge(nx_y, 2 * i + s + 1)
                after(dve, nx_ok[s], i)
                dve.scalar_tensor_tensor(tiles_of(9 + s)[0:rows, 0:tiles, :], tiles_of(6)[0:rows, 0:tiles, :], 0.0,
                                         tiles_of(2 + s)[0:rows, 0:tiles, :], ALU.max, ALU.add).then_inc(nx_used[s], 1)

            def first_norm(i, s, rows, tiles):
                scaled(i, s, rows, tiles)
                positive(i, s, rows, tiles)

            def norm_step(group, following):
                i, s, rows, tiles = group
                z = tiles_of(9 + s)[0:rows, 0:tiles, :]
                dve.wait_ge(nx_used[s], i + 1)
                dve.wait_ge(nx_e, 2 * i + s + 1)
                st.did(dve.scalar_tensor_tensor(z, tiles_of(7)[0:rows, 0:tiles, :], -1.0, z, ALU.add, ALU.add))
                st.wait()
                row_stats(z, rows, tiles, nx_v)
                if following:
                    scaled(*following)
                dve.wait_ge(nx_r, 2 * i + s + 1)
                scale, shift = (affine[0:rows, s, k, 0:tiles] for k in range(2))
                st.did(dve.reciprocal(scale, rstd[0:rows, 1, 0:tiles]))
                st.wait()
                dve.scalar_tensor_tensor(shift, bn2[0:rows, 0:tiles, 0], -1.0, scale, ALU.mult, ALU.mult).then_inc(nx_n, 1)
                if following:
                    dve.wait_ge(nx_n, 2 * i + s + 1)
                    positive(*following)
            node_steps(dve, first_norm, norm_step, st)
            end_stage(dve, 4)

            for l in range(LAYERS):
                r = rel[l]
                rows_h = lambda s: tiles_of(4 + s)[:, 0:EG, :]
                st.did(dve.memset(rows_h(1)[:, EG - 1, :], 0.0))
                st.wait()

                def stage_coefficients(i, s):
                    at = bass.ds((2 * i + s) * EG, EG)
                    dve.tensor_copy(coef_st[:, s, :, 0:BASES], coef[:, l, at, :])
                    dve.tensor_copy(coef_st[:, s, :, BASES], cont[:, at]).then_inc(coef_ok, 1)

                def messages(i, s, following):
                    dve.wait_ge(coef_ok, l * EGROUPS + 2 * i + s + 1)
                    marks = {}

                    def term(t, b):
                        y = psum[2 + (s * EG + t) % YBANKS][:, b * D:(b + 1) * D]
                        o = rows_h(s)[:, t, :]
                        if b == 1:
                            dve.wait_ge(first_ok, l * ET + 2 * EG * i + s * EG + t + 1)
                        else:
                            st.wait(marks[t, b - 1])
                        ins = dve.scalar_tensor_tensor(o, y, coef_st[:, s, t, b:b + 1], o, ALU.mult, ALU.add)
                        if b < BASES - 1:
                            st.did(ins)
                            marks[t, b] = st.n
                        else:
                            ins.then_inc(y_used, 1)

                    def run_sum(t):
                        o = rows_h(s)[:, t, :]
                        prev = rows_h(s)[:, t - 1, :] if t else rows_h(1 - s)[:, EG - 1, :]
                        dve.wait_ge(y_used, l * ET + 2 * EG * i + s * EG + t + 1)
                        if t:
                            st.wait(marks[t - 1])
                        else:
                            after(dve, r["row"][1 - s], i + s)
                        ins = dve.scalar_tensor_tensor(o, prev, coef_st[:, s, t, BASES:BASES + 1], o, ALU.mult, ALU.add)
                        if t < EG - 1:
                            st.did(ins)
                            marks[t] = st.n
                        else:
                            ins.then_inc(r["row"][s], 1)

                    for t in range(-1, EG):
                        if t + 1 < EG:
                            term(t + 1, 1)
                        if t >= 0:
                            term(t, 3)
                        if t + 1 < EG:
                            term(t + 1, 2)
                        if t >= 0:
                            run_sum(t)
                        if t == 1 and following:
                            stage_coefficients(*following)

                def message_pair(i):
                    messages(i, 0, (i, 1))
                    messages(i, 1, (i + 1, 0))
                stage_coefficients(0, 0)
                in_pairs(dve, message_pair, EITER - 1, st)
                messages(EITER - 1, 0, (EITER - 1, 1))
                messages(EITER - 1, 1, None)
                dve.wait_ge(fix_in, 16 * (2 + l))
                dve.wait_ge(fix_mm, 3 + l)
                dve.tensor_tensor(fix[:, 1, 0:D], fix[:, 0, 0:D], psum[0][:, 0:D], ALU.add).then_inc(fixed, 1)
                end_stage(dve, 5 + 2 * l)

                def update(i, s, rows, tiles):
                    dve.wait_ge(r["n_row"][s], NODE_ROUND * i + 16 * tiles)
                    after(dve, r["nh_ok" if l == 0 else "h_ok"][s], i)
                    for c, t0, n in chunks(tiles):
                        b = c % 2
                        dve.wait_ge(r["nm_ps"][b], 4 * i + 2 * s + c // 2 + 1)
                        dve.tensor_tensor(work[10 + s][0:rows, t0 * D:(t0 + n) * D], psum[2 + c][0:rows, 0:n * D],
                                          work[s][0:rows, t0 * D:(t0 + n) * D], ALU.add).then_inc(r["nm_used"][b], 1)
                    wait_group(dve, r["nm_used"], i, s, tiles)
                    dve.sem_inc(r["s_ok"][s], 1)

                def update_step(group, following):
                    i, s, rows, tiles = group
                    z = tiles_of(12 + s)[0:rows, 0:tiles, :]
                    dve.wait_ge(r["n_in"][s], 32 * (i + 1))
                    dve.wait_ge(r["h_ok"][s], i + 1)
                    dve.tensor_tensor(z, z, tiles_of(4 + s)[0:rows, 0:tiles, :], ALU.add).then_inc(r["z_ok"][s], 1)
                    dve.wait_ge(r["z_ok"][s], i + 1)
                    row_stats(z, rows, tiles, r["v_ok"])
                    if following:
                        update(*following)
                    norm_rows(z, tiles_of(6 + s)[0:rows, 0:tiles, :], rows, tiles, r["r_ok"], 2 * i + s + 1,
                              (r["nh_out"][s], 16 * i), r["nh_ok"][s])
                if l == 0:
                    def update_pair(i):
                        for s in range(2):
                            update(i, s, P, NT)
                            coefficients(1, bass.ds((2 * i + s) * CT, CT), CT, (4, 12, 13))
                    in_pairs(dve, update_pair, LAST, st)
                    update(LAST, 0, TAIL, 1)
                else:
                    node_steps(dve, update, update_step, st)
                end_stage(dve, 6 + 2 * l)


_INS = ['x', 'src', 'dst', 'edge_type_32', 'L0_gnn_Wl', 'L0_gnn_Wr', 'L0_gnn_att', 'L0_gnn_bias_conv',
        'L0_gnn_gn_weight', 'L0_gnn_gn_bias', 'L0_gnn_gn_mean_scale', 'L1_gnn_basis', 'L1_gnn_comp',
        'L1_gnn_loop_w', 'L1_gnn_bias']


def kernel(**inputs):
    import numpy as _np
    import concourse.bacc as _bacc
    from concourse import mybir as _mybir
    from concourse.bass_utils import run_bass_kernel_spmd as _run

    nc = _bacc.Bacc("TRN2", target_bir_lowering=False, num_devices=1)
    arrays, args = {}, []
    for name in _INS:
        a = _np.ascontiguousarray(inputs[name])
        arrays[f"in_{name}_dram"] = a
        args.append(nc.dram_tensor(f"in_{name}_dram", a.shape, _mybir.dt.from_np(a.dtype), kind="ExternalInput").ap())
    args.append(nc.dram_tensor("out_0_dram", (N, D), _mybir.dt.float32, kind="ExternalOutput").ap())
    gnn_kernel(nc, *args)
    r = _run(nc, [arrays], core_ids=[0])
    return r.results[0]["out_0_dram"]
```
